# Optimizing a Trainium2 kernel written in Bass

```python
import numpy as np
import jax
import jax.numpy as jnp

def _softmax(x, axis=-1):
    return jax.nn.softmax(x, axis=axis)

def _gelu(x):
    return jax.nn.gelu(x, approximate=True)

def _silu(x):
    return jax.nn.silu(x)

def _sigmoid(x):
    return jax.nn.sigmoid(x)

def _layernorm(x, axis=-1, eps=1e-05):
    m = jnp.mean(x, axis=axis, keepdims=True)
    v = jnp.var(x, axis=axis, keepdims=True)
    return (x - m) / jnp.sqrt(v + eps)

def _scatter_add(tgt, idx, src, axis=0):
    return tgt.at[idx].add(src)

def _segment_sum(src, seg, n):
    return jax.ops.segment_sum(src, seg, n)
kernel_name = 'mk_adaln_d1_jaxref_r8_f9d887'

def setup_inputs(seed: int=0):
    np.random.seed(seed)
    _w = jnp.asarray

    def _L0_attn_setup():
        import jax, jax.numpy as jnp
        import numpy as np
        B, T, C = (4, 256, 256)
        N, K = (16, 4)
        G, H = (N // K, C // N)

        def _rmsnorm(x):
            var = jnp.mean(jnp.square(x.astype(jnp.float32)), axis=-1, keepdims=True)
            return (x * jax.lax.rsqrt(var + 1e-06)).astype(x.dtype)

        def _sine_table(features, length, max_timescale=10000.0):
            fraction = jnp.arange(0, features, 2, dtype=jnp.float32) / features
            timescale = max_timescale ** fraction
            sinusoid = jnp.einsum('i,j->ij', jnp.arange(length).astype(jnp.float32), 1.0 / timescale, precision=jax.lax.Precision.HIGHEST)
            sinusoid = jnp.concatenate([sinusoid, sinusoid], axis=-1)
            return (jnp.sin(sinusoid), jnp.cos(sinusoid))

        def _rotate_half(x):
            x1, x2 = jnp.split(x, 2, axis=-1)
            return jnp.concatenate([-x2, x1], axis=-1)
        key = jax.random.key(seed)
        kx, kq, kk, kv, ko = jax.random.split(key, 5)
        q_std = float(np.sqrt(2.0 / (5.0 * C)))
        o_std = 2.0 / 24 / float(np.sqrt(N * H))
        return {'x': jax.random.normal(kx, (B, T, C), dtype=jnp.float32), 'Wq': jax.random.normal(kq, (C, N * H), dtype=jnp.float32) * q_std, 'Wk': jax.random.normal(kk, (C, K * H), dtype=jnp.float32) * q_std, 'Wv': jax.random.normal(kv, (C, K * H), dtype=jnp.float32) * q_std, 'Wout': jax.random.normal(ko, (N * H, C), dtype=jnp.float32) * o_std}
    _L0_attn_in = _L0_attn_setup()

    def _L0_ffn_setup():
        import jax, jax.numpy as jnp
        import numpy as np
        B, S, H = (2, 64, 256)
        E, G, TOPK_G, K = (64, 8, 4, 6)
        I = 64
        SH_I = 256
        RSF = 2.5

        def relu2(x):
            r = jax.nn.relu(x)
            return r * r
        key = jax.random.key(seed)
        ks = jax.random.split(key, 7)
        s = lambda d: 1.0 / np.sqrt(d)
        return {'hidden_states': jax.random.normal(ks[0], (B, S, H), jnp.float32), 'gate_w': jax.random.normal(ks[1], (E, H), jnp.float32) * s(H), 'gate_bias': jax.random.normal(ks[2], (E,), jnp.float32) * 0.01, 'w1': jax.random.normal(ks[3], (E, I, H), jnp.float32) * s(H), 'w2': jax.random.normal(ks[4], (E, H, I), jnp.float32) * s(I), 'shared_up': jax.random.normal(ks[5], (SH_I, H), jnp.float32) * s(H), 'shared_down': jax.random.normal(ks[6], (H, SH_I), jnp.float32) * s(SH_I)}
    _L0_ffn_in = _L0_ffn_setup()
    _L0_c = _w((lambda *s: np.random.randn(*s).astype(np.float32) * 0.05)(4, 256))
    _L0_wmod = _w((lambda *s: np.random.randn(*s).astype(np.float32) * 0.05)(256, 6 * 256) * 256 ** (-0.5))
    _d = {'L0_attn_x': _L0_attn_in['x'], 'L0_attn_Wq': _L0_attn_in['Wq'], 'L0_attn_Wk': _L0_attn_in['Wk'], 'L0_attn_Wv': _L0_attn_in['Wv'], 'L0_attn_Wout': _L0_attn_in['Wout'], 'L0_ffn_gate_w': _L0_ffn_in['gate_w'], 'L0_ffn_gate_bias': _L0_ffn_in['gate_bias'], 'L0_ffn_w1': _L0_ffn_in['w1'], 'L0_ffn_w2': _L0_ffn_in['w2'], 'L0_ffn_shared_up': _L0_ffn_in['shared_up'], 'L0_ffn_shared_down': _L0_ffn_in['shared_down'], 'L0_c': _L0_c, 'L0_wmod': _L0_wmod}
    _x0 = _d['L0_attn_x']
    _d['L0_attn_x'] = jax.random.normal(jax.random.fold_in(jax.random.key(seed), 1), (4, 1024, 256), dtype=_x0.dtype)
    del _x0
    return _d

def reference(L0_attn_x, L0_attn_Wq, L0_attn_Wk, L0_attn_Wv, L0_attn_Wout, L0_ffn_gate_w, L0_ffn_gate_bias, L0_ffn_w1, L0_ffn_w2, L0_ffn_shared_up, L0_ffn_shared_down, L0_c, L0_wmod):

    def _L0_attn_ref(x, Wq, Wk, Wv, Wout):
        import jax, jax.numpy as jnp
        import numpy as np
        B, T, C = (4, 256, 256)
        N, K = (16, 4)
        G, H = (N // K, C // N)

        def _rmsnorm(x):
            var = jnp.mean(jnp.square(x.astype(jnp.float32)), axis=-1, keepdims=True)
            return (x * jax.lax.rsqrt(var + 1e-06)).astype(x.dtype)

        def _sine_table(features, length, max_timescale=10000.0):
            fraction = jnp.arange(0, features, 2, dtype=jnp.float32) / features
            timescale = max_timescale ** fraction
            sinusoid = jnp.einsum('i,j->ij', jnp.arange(length).astype(jnp.float32), 1.0 / timescale, precision=jax.lax.Precision.HIGHEST)
            sinusoid = jnp.concatenate([sinusoid, sinusoid], axis=-1)
            return (jnp.sin(sinusoid), jnp.cos(sinusoid))

        def _rotate_half(x):
            x1, x2 = jnp.split(x, 2, axis=-1)
            return jnp.concatenate([-x2, x1], axis=-1)
        b, t, c = x.shape
        q = _rmsnorm(x @ Wq)
        k = _rmsnorm(x @ Wk)
        v = x @ Wv
        q = q.reshape(b, t, K, G, H)
        k = k.reshape(b, t, K, H)
        v = v.reshape(b, t, K, H)
        sin, cos = _sine_table(H, t)
        qcos, qsin = (cos[None, :, None, None, :], sin[None, :, None, None, :])
        kcos, ksin = (cos[None, :, None, :], sin[None, :, None, :])
        q = (q * qcos + _rotate_half(q) * qsin).astype(q.dtype)
        k = (k * kcos + _rotate_half(k) * ksin).astype(k.dtype)
        scale = jax.lax.rsqrt(jnp.array(H, dtype=jnp.float32)).astype(q.dtype)
        q = q * scale
        logits = jnp.einsum('btkgh,bskh->bkgts', q, k)
        probs = jax.nn.softmax(logits.astype(jnp.float32), axis=-1).astype(logits.dtype)
        enc = jnp.einsum('bkgts,bskh->btkgh', probs, v)
        return enc.reshape(b, t, N * H) @ Wout

    def _L0_ffn_ref(hidden_states, gate_w, gate_bias, w1, w2, shared_up, shared_down):
        import jax, jax.numpy as jnp
        import numpy as np
        B, S, H = (2, 64, 256)
        E, G, TOPK_G, K = (64, 8, 4, 6)
        I = 64
        SH_I = 256
        RSF = 2.5

        def relu2(x):
            r = jax.nn.relu(x)
            return r * r
        x = hidden_states.reshape(-1, H)
        T = x.shape[0]
        logits = jnp.dot(x.astype(jnp.float32), gate_w.astype(jnp.float32).T)
        scores = jax.nn.sigmoid(logits)
        scores_b = scores + gate_bias
        sb_g = scores_b.reshape(T, G, E // G)
        group_scores = jnp.sum(jax.lax.top_k(sb_g, 2)[0], axis=-1)
        grp_idx = jax.lax.top_k(group_scores, TOPK_G)[1]
        grp_mask = jnp.sum(jax.nn.one_hot(grp_idx, G, dtype=jnp.float32), axis=1)
        expert_mask = jnp.repeat(grp_mask, E // G, axis=-1) > 0
        masked = jnp.where(expert_mask, scores_b, -jnp.inf)
        _, top_idx = jax.lax.top_k(masked, K)
        topw = jnp.take_along_axis(scores, top_idx, axis=1)
        topw = topw / (jnp.sum(topw, axis=-1, keepdims=True) + 1e-20) * RSF
        w_dense = jnp.zeros((T, E), jnp.float32).at[jnp.arange(T)[:, None], top_idx].add(topw)
        h = relu2(jnp.einsum('th,eih->tei', x, w1))
        h = h * w_dense[:, :, None]
        routed = jnp.einsum('tei,ehi->th', h, w2)
        shared = jnp.dot(relu2(jnp.dot(x, shared_up.T)), shared_down.T)
        out = (routed + shared).astype(hidden_states.dtype)
        return out.reshape(hidden_states.shape)
    x = L0_attn_x
    mod = (_silu(L0_c) @ L0_wmod).reshape(L0_c.shape[0], 6, 1, -1)
    sa, ca, ga, sb, cb, gb = (mod[:, 0], mod[:, 1], mod[:, 2], mod[:, 3], mod[:, 4], mod[:, 5])
    ga = (2 * (ga >= 0) - 1) * jnp.maximum(jnp.abs(ga), 0.25)
    gb = (2 * (gb >= 0) - 1) * jnp.maximum(jnp.abs(gb), 0.25)
    h = _layernorm(x, axis=-1) * (1 + ca) + sa
    x = x + ga * _L0_attn_ref(h, L0_attn_Wq, L0_attn_Wk, L0_attn_Wv, L0_attn_Wout)
    h = _layernorm(x, axis=-1) * (1 + cb) + sb
    x = x + gb * _L0_ffn_ref(h, L0_ffn_gate_w, L0_ffn_gate_bias, L0_ffn_w1, L0_ffn_w2, L0_ffn_shared_up, L0_ffn_shared_down)
    return x

_drawn_inputs = setup_inputs


def setup_inputs(seed=0):
    import zlib

    import numpy as np

    out = dict(_drawn_inputs(seed))
    spreads = {}
    factors = {'L0_attn_Wq': 6.601, 'L0_attn_Wk': 6.057, 'L0_attn_Wv': 6.001, 'L0_attn_Wout': 5.68}
    for name, (base, spread) in spreads.items():
        noise = np.random.default_rng([zlib.crc32(name.encode()), seed]).standard_normal(out[name].shape)
        drawn = base * np.exp(spread * noise) if base else spread * noise
        out[name] = jnp.asarray(drawn.astype(out[name].dtype))
    for name, factor in factors.items():
        out[name] = (out[name] * factor).astype(out[name].dtype)
    return out
```

```python
from contextlib import ExitStack

import numpy as np

import concourse.bass as bass
from concourse import mybir

F32 = mybir.dt.float32
BF16 = mybir.dt.bfloat16
ALU = mybir.AluOpType
ACT = mybir.ActivationFunctionType
AX = mybir.AxisListType

P = 128
B, T, C = 4, 1024, 256
NT = T // P
CK = C // P
NH, NKV, HD = 16, 4, 16
G = NH // NKV
NQK = NH + NKV
QKV = (NH + 2 * NKV) * HD
HALF = HD // 2
PARTS = 6
KS = PARTS * HD
E, NG, TOPG, TOPK = 64, 8, 4, 6
EG = E // NG
EI = 64
SH = 256
RSF = 2.5
TH = 512
NTH = T // TH
TPH = TH // P
HB = 4
NHB = NT // HB
NSH = SH // P
NCH = E * EI // P
NQ = NSH + NCH
RING = 4
UNROLL = RING
FREE = 2
MODS = (0, 1, 3, 4)
STEPS = NTH * NKV * NT
MASKED, SENTINEL, CHOSEN = -3.0e38, -3.2e38, 3.0e38
LN_EPS, RMS_EPS, SUM_EPS = 1e-5, 1e-6, 1e-20


def hold(eng, held, sem, value):
    eng.wait_ge(sem, value)
    eng.sem_inc(held, 1)


class Chain:

    def __init__(self, eng, sem, held, base=0, row=None, per=0):
        self.eng, self.sem, self.held, self.base, self.row, self.per = eng, sem, held, base, row, per
        self.n = 0

    def add(self, ins):
        ins.then_inc(self.sem, 1)
        self.n += 1

    def settle(self, apart=False):
        k = self.base + self.n
        if self.row is not None:
            k = self.row * self.per + k
        if apart:
            hold(self.eng, self.held, self.sem, k)
        else:
            self.eng.wait_ge(self.sem, k)

    def step(self, ins, apart=False):
        self.add(ins)
        self.settle(apart)


DVE_ROW = 156
POOL_ROW = 12


def adaln_layer(nc, x, cT, wmod, wq, wk, wv, wout, gate_w, gate_bias, w1, w2, up, down, cos, sin,
                eye, before, out):
    wT = nc.dram_tensor("gate_weights_T", [E, T], F32, kind="Internal").ap()

    with ExitStack() as ctx:
        def sb(name, shape, dt=F32):
            return ctx.enter_context(nc.sbuf_tensor(name, shape, dt))

        def sem(name):
            return ctx.enter_context(nc.semaphore(name))

        psum = ctx.enter_context(nc.psum_tensor("psum", [P, 8, 512], F32))

        ident = sb("ident", [P, P])
        ident_b = sb("ident_b", [P, P], BF16)
        cos_sb, sin_sb = sb("cos_sb", [P, NT, HALF]), sb("sin_sb", [P, NT, HALF])
        before_sb = sb("before_sb", [P, NG, NG])
        bias_sb = sb("bias_sb", [P, E])
        wqkv_sb = sb("wqkv_sb", [P, CK, QKV])
        wout_sb = sb("wout_sb", [P, NKV, C])
        gate_sb = sb("gate_sb", [P, CK, E])
        minus_half = sb("minus_half", [P, 2 * NT])
        c_sb = sb("c_sb", [P, CK, B])
        silu = sb("silu", [P, CK, B])
        modcol = sb("modcol", [P, len(MODS) * CK, B])
        modrow = sb("modrow", [P, 2, B, C])
        xs = sb("xs", [P, B * NT, C])
        stats = sb("stats", [P, NT, 6])
        mv = sb("mv", [P, NT, 2])
        rstd = sb("rstd", [P, NT])
        curmod = sb("curmod", [P, len(MODS) * CK])
        xn = sb("xn", [P, NT, C])
        hT = sb("hT", [P, CK, T])
        qkv = sb("qkv", [P, HB, QKV])
        ssq = sb("ssq", [P, NT, 2])
        rrms = sb("rrms", [P, NT, 2])
        rope = [sb(f"rope{i}", [P, HB, NQK, HALF]) for i in range(4)]
        rot = sb("rot", [P, HB, NQK, HD])
        rest = sb("rest", [P, HB, NQK, HD])
        stack = sb("stack", [P, HB, NQK, PARTS, HD], BF16)
        QT = sb("QT", [KS, NH, T], BF16)
        KT = sb("KT", [KS, NKV, T], BF16)
        V1 = sb("V1", [P, NT, NKV, 2 * HD])
        probs = sb("probs", [P, 3, G, TH])
        o_sb = sb("o_sb", [P, 2, TH])
        o_den = sb("o_den", [P, TH])
        encT = sb("encT", [P, NKV, T])
        squares = o_den[:, 0:NH * HD]
        gated_y = sb("gated_y", [P, 2, C])
        w1_ring = sb("w1_ring", [P, RING, CK, P])
        w2_ring = sb("w2_ring", [P, RING, C])
        flat = probs[:, :, :, :].rearrange("p a g t -> p (a g t)")
        wmod_sb = flat[:, 0:CK * 6 * C].rearrange("p (k n) -> p k n", k=CK)
        siluB = flat[:, CK * 6 * C:CK * 6 * C + CK * B * P].rearrange("p (k b n) -> p k b n", k=CK, b=B)
        gw_ring = flat[:, 0:RING * T].rearrange("p (s t) -> p s t", s=RING)
        hid = flat[:, RING * T:(RING + 2) * T].rearrange("p (s g t) -> p s g t", s=2, g=NTH)
        relu_w = xn[:, :, :].rearrange("p t c -> p (t c)")[:, 0:T].rearrange("p (g t) -> p g t", g=NTH)
        wT_sb = encT[0:E, 0, :]
        rowtmp = encT[:, 0:2, :].rearrange("p a t -> p (a t)")
        rflat = rot[:, :, :, :].rearrange("p a h d -> p (a h d)")
        scores = rflat[:, 0:NT * E]
        sbias = rflat[:, NT * E:2 * NT * E]
        VW = E + 2
        restf = rest[:, :, :, :].rearrange("p a h d -> p (a h d)")
        cand = restf[:, 0:NT * VW].rearrange("p (t v) -> p t v", t=NT)
        wdense = restf[:, NT * VW:NT * (VW + E)].rearrange("p (t e) -> p t e", t=NT)
        tmp = [r[:, :, :, :].rearrange("p a h d -> p (a h d)") for r in rope]

        x_loaded = sem("x_loaded")
        w_loaded = sem("w_loaded")
        wmod_loaded = sem("wmod_loaded")
        zeros_set = sem("zeros_set")
        dve_chain = sem("dve_chain")
        pool_chain = sem("pool_chain")
        held = sem("held")
        held_pool = sem("held_pool")
        held_sp = sem("held_sp")
        held_pe = sem("held_pe")
        consts_set = sem("consts_set")
        silu_exp = sem("silu_exp")
        silu_ready = sem("silu_ready")
        mod_cols = sem("mod_cols")
        mod_rows = sem("mod_rows")
        mod_done = sem("mod_done")
        stats_ready = sem("stats_ready")
        rstd_ready = sem("rstd_ready")
        xn_ready = sem("xn_ready")
        xnT_ready = sem("xnT_ready")
        hT_ready = sem("hT_ready")
        qkv_psum = sem("qkv_psum")
        qkv_copied = sem("qkv_copied")
        squares_ready = sem("squares_ready")
        rrms_ready = sem("rrms_ready")
        rot_done = sem("rot_done")
        parts_ready = sem("parts_ready")
        q_stacked = sem("q_stacked")
        k_stacked = sem("k_stacked")
        v_ready = sem("v_ready")
        stackT_psum = sem("stackT_psum")
        stackT_dve = sem("stackT_dve")
        stackT_act = sem("stackT_act")
        logits_ready = sem("logits_ready")
        exp_done = sem("exp_done")
        pv_done = sem("pv_done")
        o_copied = sem("o_copied")
        enc_ready = sem("enc_ready")
        y_psum = sem("y_psum")
        y_read = sem("y_read")
        logit_psum = sem("logit_psum")
        escore = sem("escore")
        w_ready = sem("w_ready")
        wT_psum = sem("wT_psum")
        wT_copied = sem("wT_copied")
        wT_stored = sem("wT_stored")
        chunk_loaded = [sem(f"chunk_loaded{s}") for s in range(RING)]
        gw_loaded = [sem(f"gw_loaded{s}") for s in range(RING)]
        h_psum = sem("h_psum")
        weighted = sem("weighted")
        hid_ready = sem("hid_ready")
        chunk_used = sem("chunk_used")
        row_done = sem("row_done")
        stored = sem("stored")

        block = ctx.enter_context(nc.Block())

        @block.sync
        def _(sp):
            sp.dma_start(c_sb[:, :, :], cT.rearrange("(k p) b -> p k b", p=P)).then_inc(wmod_loaded, 16)
            sp.dma_start(wmod_sb, wmod.rearrange("(k p) n -> p k n", p=P)).then_inc(wmod_loaded, 16)
            sp.dma_start(ident[:, :], eye).then_inc(w_loaded, 16)
            sp.dma_start(cos_sb[:, :, :], cos.rearrange("(t p) f -> p t f", p=P)).then_inc(w_loaded, 16)
            sp.dma_start(sin_sb[:, :, :], sin.rearrange("(t p) f -> p t f", p=P)).then_inc(w_loaded, 16)
            sp.dma_start(before_sb[:, :, :], before.unsqueeze(0).broadcast_to([P, NG, NG])).then_inc(w_loaded, 16)
            sp.dma_start(bias_sb[:, :], gate_bias.unsqueeze(0).broadcast_to([P, E])).then_inc(w_loaded, 16)
            sp.dma_start(wqkv_sb[:, :, 0:C], wq.rearrange("(k p) n -> p k n", p=P)).then_inc(w_loaded, 16)
            sp.dma_start(wqkv_sb[:, :, C:C + 64], wk.rearrange("(k p) n -> p k n", p=P)).then_inc(w_loaded, 16)
            sp.dma_start(wqkv_sb[:, :, C + 64:QKV], wv.rearrange("(k p) n -> p k n", p=P)).then_inc(w_loaded, 16)
            sp.dma_start(gate_sb[:, :, :], gate_w.rearrange("(k p) e -> p k e", p=P)).then_inc(w_loaded, 16)
            sp.wait_ge(zeros_set, 1)
            wo = wout.rearrange("(k g h) c -> g h k c", k=NKV, g=G)
            for g in range(G):
                sp.dma_start(wout_sb[32 * g:32 * g + HD, :, :], wo[g]).then_inc(w_loaded, 16)
            with sp.Fori(0, B) as b:
                sp.dma_start(xs[:, bass.ds(b * NT, NT), :],
                             x[bass.ds(b * T, T), :].rearrange("(t p) c -> p t c", p=P)).then_inc(x_loaded, 16)
                hold(sp, held_sp, x_loaded, b * 16 + 16)
                for q in range(NSH):
                    sp.dma_start(w1_ring[:, q + 2, :, :],
                                 up[:, q * P:(q + 1) * P].rearrange("(k p) n -> p k n", p=P)
                                 ).then_inc(chunk_loaded[q + 2], 16)
                    sp.dma_start(w2_ring[:, q + 2, :], down[q * P:(q + 1) * P, :]).then_inc(chunk_loaded[q + 2], 16)
                hold(sp, held_sp, wT_copied, b + 1)
                sp.dma_start(wT, wT_sb).then_inc(wT_stored, 16)
                hold(sp, held_sp, wT_stored, b * 16 + 16)
                with sp.Fori(0, NCH // UNROLL) as i:
                    for j in range(UNROLL):
                        hold(sp, held_sp, chunk_used, b * NQ + i * UNROLL + (NSH + j - RING + 1 + FREE))
                        sp.dma_start(w1_ring[:, j, :, :],
                                     w1[:, bass.ds(i * UNROLL * P + j * P, P)].rearrange("(k p) n -> p k n", p=P)
                                     ).then_inc(chunk_loaded[j], 16)
                        sp.dma_start(w2_ring[:, j, :], w2[bass.ds(i * UNROLL * P + j * P, P), :]
                                     ).then_inc(chunk_loaded[j], 16)
                        for k in range(2):
                            src = wT[bass.ds(i * 2 * UNROLL + (2 * j + k), 1), :].broadcast_to([EI, T])
                            sp.dma_start(gw_ring[EI * k:EI * k + EI, j, :], src).then_inc(gw_loaded[j], 16)
                for h in range(2):
                    hold(sp, held_sp, row_done, b * 2 + (h + 1))
                    n = NT // 2
                    sp.dma_start(out[bass.ds(b * T + h * (T // 2), T // 2), :].rearrange("(t p) c -> p t c", p=P),
                                 xs[:, bass.ds(b * NT + h * n, n), :]).then_inc(stored, 16)
                hold(sp, held_sp, stored, b * 32 + 32)

        @block.tensor
        def _(pe):
            def psum_b(k):
                return psum[:, k, :].bitcast(BF16)

            pe.wait_ge(wmod_loaded, 32)
            pe.wait_ge(silu_ready, 1)
            for m, mod in enumerate(MODS):
                for k in range(CK):
                    o = psum[:, 0, (m * CK + k) * B:(m * CK + k + 1) * B]
                    for c in range(CK):
                        mm = pe.matmul(o, wmod_sb[:, c, mod * C + k * P:mod * C + (k + 1) * P], silu[:, c, :],
                                       start=(c == 0), stop=(c == CK - 1))
            mm.then_inc(mod_cols, 1)
            for r, mod in enumerate((2, 5)):
                for b in range(B):
                    o = psum[:, 1 + r * 2 + b // 2, (b % 2) * C:(b % 2 + 1) * C]
                    for c in range(CK):
                        mm = pe.matmul(o, siluB[:, c, b, :], wmod_sb[:, c, mod * C:(mod + 1) * C],
                                       start=(c == 0), stop=(c == CK - 1))
            mm.then_inc(mod_rows, 1)
            pe.wait_ge(w_loaded, 16 * 13)
            pe.wait_ge(consts_set, 1)
            pe.wait_ge(mod_done, 1)
            pe.sem_inc(chunk_used, FREE)

            with pe.Fori(0, B) as b:
                def norm_transposes(which, i):
                    n = which * NT + i
                    pe.wait_ge(xn_ready, b * 2 * NT + (n + 1))
                    if i >= 2:
                        pe.wait_ge(hT_ready, b * 2 * NT + (n - 1))
                    for k in range(CK):
                        mm = pe.transpose(psum[:, i % 2, k * P:(k + 1) * P], xn[:, i, k * P:(k + 1) * P], ident[:, :])
                    mm.then_inc(xnT_ready, 1)

                def project(i):
                    pe.wait_ge(hT_ready, b * 2 * NT + (i + 1))
                    if i >= 2:
                        pe.wait_ge(qkv_copied, b * NT + (i - 1))
                    for k in range(CK):
                        mm = pe.matmul(psum[:, 2 + i % 2, 0:QKV], hT[:, k, i * P:(i + 1) * P], wqkv_sb[:, k, :],
                                       start=(k == 0), stop=(k == CK - 1))
                    mm.then_inc(qkv_psum, 1)

                def stack_transposes(hb):
                    for ii in range(HB):
                        i = hb * HB + ii
                        for part in range(3):
                            if ii == 0 and part == 0:
                                pe.wait_ge(q_stacked, b * NHB + (hb + 1))
                                pe.wait_ge(parts_ready, b * NHB + (hb + 1))
                            if ii == 0 and part == 2:
                                pe.wait_ge(k_stacked, b * NHB + (hb + 1))
                            if i >= 1:
                                if part == 1:
                                    pe.wait_ge(stackT_act, b * NT + i)
                                elif part == 0:
                                    pe.wait_ge(stackT_dve, b * 2 * NT + (2 * i - 1))
                                else:
                                    pe.wait_ge(stackT_dve, b * 2 * NT + 2 * i)
                            n = 8 if part < 2 else NKV
                            for h in range(n):
                                mm = pe.transpose(psum_b(4 + part)[0:KS, h * P:(h + 1) * P],
                                                  stack[:, ii, part * 8 + h, :, :].rearrange("p a d -> p (a d)"),
                                                  ident_b[:, :])
                            mm.then_inc(stackT_psum, 1)

                for hb in range(NHB):
                    for i in range(hb * HB, (hb + 1) * HB):
                        norm_transposes(0, i)
                        project(i)
                    stack_transposes(hb)

                def logits(st, pair):
                    th, kv, s = st // (NKV * NT), st // NT % NKV, st % NT
                    n = 2 * st + pair
                    if n >= 3:
                        pe.wait_ge(exp_done, b * 2 * STEPS + (n - 2))
                    for k in range(2):
                        mm = pe.matmul(psum[:, 2 * (n % 3) + k, :], KT[:, kv, s * P:(s + 1) * P],
                                       QT[:, kv * G + 2 * pair + k, th * TH:(th + 1) * TH], start=True, stop=True)
                    mm.then_inc(logits_ready, 1)

                def attend(st):
                    kv, s = st // NT % NKV, st % NT
                    pe.wait_ge(exp_done, b * 2 * STEPS + (2 * st + 2))
                    if s == 0 and st >= NT:
                        pe.wait_ge(o_copied, b * NTH * NKV + st // NT)
                    for g in range(G):
                        mm = pe.matmul(psum[32 * g:32 * g + 32, 6, :], V1[:, s, kv, :], probs[:, st % 3, g, :],
                                       start=(s == 0), stop=(s == NT - 1))
                    mm.then_inc(pv_done, 1)

                def project_out(i):
                    pe.wait_ge(enc_ready, b * NTH * NKV + (i // TPH + 1) * NKV)
                    if i >= 1:
                        pe.wait_ge(y_read, b * NT + i)
                    for kv in range(NKV):
                        mm = pe.matmul(psum[:, 7, (i % 2) * C:(i % 2 + 1) * C], encT[:, kv, i * P:(i + 1) * P],
                                       wout_sb[:, kv, :], start=(kv == 0), stop=(kv == NKV - 1))
                    mm.then_inc(y_psum, 1)

                pe.wait_ge(stackT_act, b * NT + NT)
                pe.wait_ge(stackT_dve, b * 2 * NT + 2 * NT)
                pe.wait_ge(v_ready, b * NHB + NHB)
                for st in range(STEPS + 1):
                    if st < STEPS:
                        logits(st, 0)
                        logits(st, 1)
                    if st >= 1:
                        attend(st - 1)
                    r = st - NKV * NT - 3
                    if r >= 0 and r < TPH:
                        project_out(r)
                for i in range(TPH, NT):
                    project_out(i)

                for i in range(NT):
                    norm_transposes(1, i)
                for i in range(NT):
                    pe.wait_ge(hT_ready, b * 2 * NT + (NT + i + 1))
                    for k in range(CK):
                        mm = pe.matmul(psum[:, 2, i * E:(i + 1) * E], hT[:, k, i * P:(i + 1) * P], gate_sb[:, k, :],
                                       start=(k == 0), stop=(k == CK - 1))
                mm.then_inc(logit_psum, 1)

                def up_chunk(slot, hslot, first, row_q, chunks_before):
                    for g in range(NTH):
                        if not first:
                            pe.wait_ge(hid_ready, row_q * 2 + (g - 1))
                        if g == 0:
                            pe.wait_ge(chunk_loaded[slot], chunks_before * 32 + 32)
                        for k in range(CK):
                            mm = pe.matmul(psum[:, g, :], w1_ring[:, slot, k, :], hT[:, k, g * TH:(g + 1) * TH],
                                           start=(k == 0), stop=(k == CK - 1))
                        mm.then_inc(h_psum, 1)

                def down_chunk(slot, hslot, first, row_q):
                    for i in range(NT):
                        if i % TPH == 0:
                            pe.wait_ge(hid_ready, row_q * 2 + (i // TPH + 1))
                        mm = pe.matmul(psum[:, 4 + i // 2, (i % 2) * C:(i % 2 + 1) * C],
                                       hid[:, hslot, i // TPH, (i % TPH) * P:(i % TPH + 1) * P], w2_ring[:, slot, :],
                                       start=(first and i % 2 == 0), stop=True, skip_group_check=True)
                    mm.then_inc(chunk_used, 1)

                turns = NCH // UNROLL
                up_chunk(2, 0, True, b * NQ, b * (turns + 1))
                up_chunk(3, 1, False, b * NQ + 1, b * (turns + 1))
                down_chunk(2, 0, True, b * NQ)
                hold(pe, held_pe, w_ready, b + 1)
                for i in range(NT):
                    mm = pe.transpose(psum[0:E, 2 + i // TPH, (i % TPH) * P:(i % TPH + 1) * P],
                                      wdense[:, i, :], ident[:, :])
                mm.then_inc(wT_psum, 1)
                with pe.Fori(0, turns) as i:
                    for j in range(UNROLL):
                        before_j = b * turns + i if j < 2 else b * (turns + 1) + i + 1
                        up_chunk(j, j % 2, False, b * NQ + i * UNROLL + (NSH + j), before_j)
                        down_chunk((j - 1) % RING, 1 - j % 2, False, b * NQ + i * UNROLL + (NSH + j - 1))
                down_chunk(3, 1, False, b * NQ + (NQ - 1))

        @block.scalar
        def _(act):
            act.wait_ge(wmod_loaded, 32)
            act.activation(silu[:, :, :], c_sb[:, :, :], ACT.Exp, scale=-1.0).then_inc(silu_exp, 1)
            with act.Fori(0, B) as b:
                def modulate(which, i):
                    n = which * NT + i
                    act.wait_ge(xnT_ready, b * 2 * NT + (n + 1))
                    if i == 0:
                        act.wait_ge(stats_ready, b * 2 + (which + 1))
                    for k in range(CK):
                        m = 2 * which * CK + k
                        a = act.activation(hT[:, k, i * P:(i + 1) * P], psum[:, i % 2, k * P:(k + 1) * P], ACT.Identity,
                                           bias=curmod[:, m:m + 1], scale=curmod[:, m + CK:m + CK + 1])
                    a.then_inc(hT_ready, 1)

                for hb in range(NHB):
                    for ii in range(HB):
                        modulate(0, hb * HB + ii)
                    for ii in range(HB):
                        i = hb * HB + ii
                        act.wait_ge(qkv_copied, b * NT + (i + 1))
                        act.activation(squares[:, 0:NH * HD], qkv[:, ii, 0:NH * HD], ACT.Square,
                                       accum_out=ssq[:, i, 0:1]).then_inc(squares_ready, 1)
                        act.wait_ge(squares_ready, b * 2 * NT + (2 * i + 1))
                        act.activation(squares[:, 0:NKV * HD], qkv[:, ii, NH * HD:NQK * HD], ACT.Square,
                                       accum_out=ssq[:, i, 1:2]).then_inc(squares_ready, 1)
                        act.wait_ge(squares_ready, b * 2 * NT + (2 * i + 2))
                    act.wait_ge(parts_ready, b * NHB + (hb + 1))
                    for src, dst in ((0, 1), (0, 3), (5, 2)):
                        a = act.activation(stack[:, :, 0:NH, dst, :], stack[:, :, 0:NH, src, :], ACT.Copy)
                    a.then_inc(q_stacked, 1)
                    for ii in range(HB):
                        i = hb * HB + ii
                        act.wait_ge(stackT_psum, b * 3 * NT + (3 * i + 2))
                        act.activation(QT[:, 8:16, i * P:(i + 1) * P],
                                       psum[:, 5, :].bitcast(BF16)[0:KS, :].rearrange("p (h t) -> p h t", h=8),
                                       ACT.Copy).then_inc(stackT_act, 1)
                for st in range(STEPS):
                    for pair in range(2):
                        n = 2 * st + pair
                        act.wait_ge(logits_ready, b * 2 * STEPS + (n + 1))
                        if st >= 3 and pair == 0:
                            act.wait_ge(pv_done, b * STEPS + (st - 2))
                        act.activation(probs[:, st % 3, 2 * pair:2 * pair + 2, :], psum[:, 2 * (n % 3):2 * (n % 3) + 2, :],
                                       ACT.Exp).then_inc(exp_done, 1)
                for i in range(NT):
                    modulate(1, i)
                act.wait_ge(logit_psum, b + 1)
                act.activation(scores, psum[:, 2, :], ACT.Exp, scale=-1.0).then_inc(escore, 1)

        @block.gpsimd
        def _(pool):
            pool.memset(wout_sb[:, :, :], 0.0).then_inc(zeros_set, 1)
            pool.memset(V1[:, :, :, HD:2 * HD], 1.0)
            pool.memset(minus_half[:, :], -0.5).then_inc(consts_set, 1)
            pool.wait_ge(consts_set, 1)
            with pool.Fori(0, B) as b:
                ch = Chain(pool, pool_chain, held_pool, 0, b, POOL_ROW)

                def rstd_of(which):
                    hold(pool, held_pool, stats_ready, b * 2 + (which + 1))
                    ch.step(pool.tensor_scalar(rstd[:, :], mv[:, :, 1], LN_EPS, None, ALU.add))
                    pool.tensor_tensor(rstd[:, :], rstd[:, :], minus_half[:, 0:NT], ALU.pow).then_inc(rstd_ready, 1)

                rstd_of(0)
                for hb in range(NHB):
                    t = slice(hb * HB, (hb + 1) * HB)
                    hold(pool, held_pool, squares_ready, b * 2 * NT + (hb + 1) * 2 * HB)
                    ch.add(pool.tensor_scalar(rrms[:, t, 0], ssq[:, t, 0], 1.0 / (NH * HD), RMS_EPS, ALU.mult, ALU.add))
                    ch.step(pool.tensor_scalar(rrms[:, t, 1], ssq[:, t, 1], 1.0 / (NKV * HD), RMS_EPS, ALU.mult, ALU.add))
                    ch.step(pool.tensor_tensor(rrms[:, t, :], rrms[:, t, :],
                                               minus_half[:, 0:2 * HB].rearrange("p (t k) -> p t k", k=2), ALU.pow),
                            apart=True)
                    pool.tensor_scalar(rrms[:, t, 0], rrms[:, t, 0], HD ** -0.5, None, ALU.mult).then_inc(rrms_ready, 1)
                    pool.tensor_copy(V1[:, t, :, 0:HD],
                                     qkv[:, :, NQK * HD:QKV].rearrange("p t (k d) -> p t k d", k=NKV)).then_inc(v_ready, 1)
                    hold(pool, held_pool, parts_ready, b * NHB + (hb + 1))
                    for src, dst in ((0, 2), (0, 4)):
                        ch.add(pool.tensor_copy(stack[:, :, NH:NQK, dst, :], stack[:, :, NH:NQK, src, :]))
                    ch.settle(apart=True)
                    pool.tensor_copy(stack[:, :, NH:NQK, 1, :], stack[:, :, NH:NQK, 5, :]).then_inc(k_stacked, 1)
                rstd_of(1)
                assert ch.n == POOL_ROW

        @block.vector
        def _(dve):
            su = Chain(dve, dve_chain, held)
            dve.wait_ge(silu_exp, 1)
            su.step(dve.tensor_scalar(silu[:, :, :], silu[:, :, :], 1.0, None, ALU.add))
            su.step(dve.reciprocal(silu[:, :, :], silu[:, :, :]))
            su.step(dve.tensor_tensor(silu[:, :, :], silu[:, :, :], c_sb[:, :, :], ALU.mult))
            su.add(dve.tensor_copy(siluB.rearrange("p k b n -> p (k b) n"),
                                   silu[:, :, :].rearrange("p k b -> p (k b)").unsqueeze(2).broadcast_to([P, CK * B, P])))
            dve.wait_ge(w_loaded, 16 * 13)
            su.add(dve.tensor_copy(ident_b[:, :], ident[:, :]))
            su.settle()
            dve.sem_inc(silu_ready, 1)
            dve.wait_ge(mod_cols, 1)
            su.step(dve.tensor_copy(modcol[:, :, :].rearrange("p m b -> p (m b)"), psum[:, 0, 0:len(MODS) * CK * B]))
            for m in (1, 3):
                v = modcol[:, m * CK:(m + 1) * CK, :]
                su.add(dve.tensor_scalar(v, v, 1.0, None, ALU.add))
            dve.wait_ge(mod_rows, 1)
            for r in range(2):
                row = modrow[:, r, :, :].rearrange("p b c -> p (b c)")
                half = rowtmp[:, r * B * C:(r + 1) * B * C]
                for a, n in ((0, half.shape[1] // 2), (1, half.shape[1] // 2)):
                    hs, rs = half[:, a * n:(a + 1) * n], row[:, a * n:(a + 1) * n]
                    g = psum[:, 1 + 2 * r + a, :]
                    su.step(dve.tensor_scalar(hs, g, 0.0, 2.0, ALU.is_ge, ALU.mult))
                    su.step(dve.tensor_scalar(hs, hs, -1.0, None, ALU.add))
                    su.step(dve.tensor_tensor(rs, hs, g, ALU.mult))
                    su.step(dve.scalar_tensor_tensor(out=rs, in0=rs, scalar=0.25, in1=hs, op0=ALU.max, op1=ALU.mult))
            dve_setup = su.n
            dve.sem_inc(mod_done, 1)

            with dve.Fori(0, B) as b:
                ch = Chain(dve, dve_chain, held, dve_setup, b, DVE_ROW)

                def xrow(i):
                    return xs[:, bass.ds(b * NT + i, 1), :].squeeze(1)

                def normalise(which):
                    for i in range(NT):
                        ch.add(dve.bn_stats(stats[:, i, :], xrow(i)))
                    ch.settle(apart=True)
                    if which == 0:
                        ch.add(dve.tensor_copy(curmod[:, :], modcol[:, :, bass.ds(b, 1)].squeeze(2)))
                    for i in range(NT):
                        ch.add(dve.bn_aggr(mv[:, i, :], stats[:, i, :]))
                    ch.settle()
                    dve.sem_inc(stats_ready, 1)
                    dve.wait_ge(rstd_ready, b * 2 + (which + 1))
                    for i in range(NT):
                        dve.tensor_scalar(xn[:, i, :], xrow(i), mv[:, i, 0:1], rstd[:, i:i + 1],
                                          ALU.subtract, ALU.mult).then_inc(xn_ready, 1)

                hold(dve, held, x_loaded, b * 16 + 16)
                normalise(0)
                for hb in range(NHB):
                    for ii in range(HB):
                        i = hb * HB + ii
                        dve.wait_ge(qkv_psum, b * NT + (i + 1))
                        if hb and ii == 0:
                            dve.wait_ge(v_ready, b * NHB + hb)
                        dve.tensor_copy(qkv[:, ii, :], psum[:, 2 + i % 2, 0:QKV]).then_inc(qkv_copied, 1)
                    dve.wait_ge(rrms_ready, b * NHB + (hb + 1))
                    for ii in range(HB):
                        i = hb * HB + ii
                        q, k = qkv[:, ii, 0:NH * HD], qkv[:, ii, NH * HD:NQK * HD]
                        ch.add(dve.tensor_scalar(q, q, rrms[:, i, 0:1], None, ALU.mult))
                        ch.add(dve.tensor_scalar(k, k, rrms[:, i, 1:2], None, ALU.mult))
                    ch.settle()
                    v = qkv[:, :, 0:NQK * HD].rearrange("p t (h d) -> p t h d", h=NQK)
                    cs = cos_sb[:, hb * HB:(hb + 1) * HB, :].unsqueeze(2).broadcast_to([P, HB, NQK, HALF])
                    sn = sin_sb[:, hb * HB:(hb + 1) * HB, :].unsqueeze(2).broadcast_to([P, HB, NQK, HALF])
                    for n, (part, tab) in enumerate(((0, cs), (1, sn), (1, cs), (0, sn))):
                        ch.add(dve.tensor_tensor(rope[n][:, :, :, :], v[:, :, :, part * HALF:(part + 1) * HALF], tab,
                                                 ALU.mult))
                    ch.settle()
                    ch.add(dve.tensor_tensor(rot[:, :, :, 0:HALF], rope[0][:, :, :, :], rope[1][:, :, :, :], ALU.subtract))
                    ch.step(dve.tensor_tensor(rot[:, :, :, HALF:HD], rope[2][:, :, :, :], rope[3][:, :, :, :], ALU.add))
                    if hb:
                        dve.wait_ge(stackT_psum, b * 3 * NT + hb * HB * 3)
                    part = [stack[:, :, :, k, :] for k in range(PARTS)]
                    r3, s3 = rot[:, :, :, :], rest[:, :, :, :]
                    ch.step(dve.tensor_copy(part[0], r3))
                    ch.step(dve.tensor_tensor(s3, r3, part[0], ALU.subtract))
                    ch.step(dve.tensor_copy(part[5], s3))
                    ch.add(dve.tensor_tensor(stack[:, :, 0:NH, 4, :], rest[:, :, 0:NH, :], stack[:, :, 0:NH, 5, :],
                                             ALU.subtract))
                    ch.step(dve.tensor_tensor(stack[:, :, NH:NQK, 3, :], rest[:, :, NH:NQK, :],
                                              stack[:, :, NH:NQK, 5, :], ALU.subtract))
                    dve.sem_inc(parts_ready, 1)
                    for ii in range(HB):
                        i = hb * HB + ii
                        dve.wait_ge(stackT_psum, b * 3 * NT + (3 * i + 1))
                        dve.tensor_copy(QT[:, 0:8, i * P:(i + 1) * P],
                                        psum[:, 4, :].bitcast(BF16)[0:KS, :].rearrange("p (h t) -> p h t", h=8)
                                        ).then_inc(stackT_dve, 1)
                        dve.wait_ge(stackT_psum, b * 3 * NT + (3 * i + 3))
                        dve.tensor_copy(KT[:, :, i * P:(i + 1) * P],
                                        psum[:, 6, :].bitcast(BF16)[0:KS, 0:NKV * P].rearrange("p (h t) -> p h t", h=NKV)
                                        ).then_inc(stackT_dve, 1)

                def divide(u):
                    th, kv = u // NKV, u % NKV
                    dve.wait_ge(pv_done, b * STEPS + (u + 1) * NT)
                    dve.tensor_copy(o_sb[:, u % 2, :], psum[:, 6, :]).then_inc(o_copied, 1)
                    hold(dve, held, o_copied, b * NTH * NKV + (u + 1))
                    ch.step(dve.stream_shuffle(o_den[:, :], o_sb[:, u % 2, :], [HD] * 32))
                    ch.step(dve.reciprocal(o_den[:, :], o_den[:, :]))
                    dve.tensor_tensor(encT[:, kv, th * TH:(th + 1) * TH], o_sb[:, u % 2, :], o_den[:, :],
                                      ALU.mult).then_inc(enc_ready, 1)

                def add_out(i):
                    dve.wait_ge(y_psum, b * NT + (i + 1))
                    dve.tensor_tensor(gated_y[:, i % 2, :], psum[:, 7, (i % 2) * C:(i % 2 + 1) * C],
                                      modrow[:, 0, bass.ds(b, 1), :].squeeze(1), ALU.mult).then_inc(y_read, 1)
                    dve.wait_ge(y_read, b * NT + (i + 1))
                    ch.add(dve.tensor_tensor(xrow(i), xrow(i), gated_y[:, i % 2, :], ALU.add))

                for u in range(NTH * NKV):
                    if u == NKV:
                        for i in range(TPH):
                            add_out(i)
                    divide(u)
                for i in range(TPH, NT):
                    add_out(i)
                ch.settle(apart=True)
                normalise(1)

                dve.wait_ge(escore, b + 1)
                ch.step(dve.tensor_scalar(scores, scores, 1.0, None, ALU.add))
                ch.step(dve.reciprocal(scores, scores))
                sc3 = scores.rearrange("p (t e) -> p t e", t=NT)
                sb3 = sbias.rearrange("p (t e) -> p t e", t=NT)
                ch.step(dve.tensor_tensor(sb3, sc3, bias_sb[:, :].unsqueeze(1).broadcast_to([P, NT, E]), ALU.add))
                sg = sbias.rearrange("p (g e) -> p g e", e=EG)
                hi = tmp[0][:, 0:NT * NG * 4].rearrange("p (g e) -> p g e", e=4)
                lo = tmp[1][:, 0:NT * NG * 4].rearrange("p (g e) -> p g e", e=4)
                ch.add(dve.tensor_tensor(hi, sg[:, :, 0:4], sg[:, :, 4:8], ALU.max))
                ch.step(dve.tensor_tensor(lo, sg[:, :, 0:4], sg[:, :, 4:8], ALU.min))
                for w, off in ((2, 0), (1, 256)):
                    mn = tmp[2][:, off:off + NT * NG * w].rearrange("p (g e) -> p g e", e=w)
                    mx = tmp[2][:, 128 + off:128 + off + NT * NG * w].rearrange("p (g e) -> p g e", e=w)
                    hi2 = tmp[3][:, off:off + NT * NG * w].rearrange("p (g e) -> p g e", e=w)
                    lo2 = tmp[3][:, 128 + off:128 + off + NT * NG * w].rearrange("p (g e) -> p g e", e=w)
                    ch.add(dve.tensor_tensor(hi2, hi[:, :, 0:w], hi[:, :, w:2 * w], ALU.max))
                    ch.add(dve.tensor_tensor(mn, hi[:, :, 0:w], hi[:, :, w:2 * w], ALU.min))
                    ch.step(dve.tensor_tensor(mx, lo[:, :, 0:w], lo[:, :, w:2 * w], ALU.max))
                    ch.step(dve.tensor_tensor(lo2, mn, mx, ALU.max))
                    hi, lo = hi2, lo2
                gs = tmp[2][:, 512:576]
                ch.step(dve.tensor_tensor(gs, hi.squeeze(2), lo.squeeze(2), ALU.add))
                gs2 = gs.rearrange("p (t g) -> p t g", t=NT)
                vi = gs2.unsqueeze(3).broadcast_to([P, NT, NG, NG])
                vj = gs2.unsqueeze(2).broadcast_to([P, NT, NG, NG])
                above = tmp[0][:, 0:512].rearrange("p (t i j) -> p t i j", t=NT, i=NG)
                equal = tmp[1][:, 0:512].rearrange("p (t i j) -> p t i j", t=NT, i=NG)
                ch.add(dve.tensor_tensor(above, vj, vi, ALU.is_gt))
                ch.step(dve.tensor_tensor(equal, vj, vi, ALU.is_equal))
                ch.step(dve.tensor_tensor(equal, equal, before_sb[:, :, :].unsqueeze(1).broadcast_to([P, NT, NG, NG]),
                                          ALU.mult))
                ch.step(dve.tensor_tensor(above, above, equal, ALU.add))
                pen = tmp[3][:, 512:576].rearrange("p (t g) -> p t g", t=NT)
                ch.step(dve.tensor_reduce(pen, above, AX.X, ALU.add))
                ch.step(dve.tensor_scalar(pen, pen, TOPG - 0.5, MASKED, ALU.is_ge, ALU.mult))
                ch.add(dve.tensor_tensor(cand[:, :, 0:E].rearrange("p t (g e) -> p t g e", g=NG),
                                         sbias.rearrange("p (t g e) -> p t g e", t=NT, g=NG),
                                         pen.unsqueeze(3).broadcast_to([P, NT, NG, EG]), ALU.add))
                ch.step(dve.memset(cand[:, :, E:VW], SENTINEL), apart=True)
                best = tmp[0][:, 512:512 + NT * 8].rearrange("p (t k) -> p t k", t=NT)
                for i in range(NT):
                    ch.add(dve.max(best[:, i, :], cand[:, i, 0:E]))
                ch.settle()
                ch.step(dve.memset(best[:, :, TOPK:8], SENTINEL), apart=True)
                for i in range(NT):
                    ch.add(dve.match_replace(cand[:, i, :], best[:, i, :], cand[:, i, :], CHOSEN))
                ch.settle()
                ch.step(dve.scalar_tensor_tensor(out=wdense, in0=cand[:, :, 0:E], scalar=0.5 * CHOSEN, in1=sc3,
                                                 op0=ALU.is_ge, op1=ALU.mult))
                total = tmp[1][:, 512:512 + NT]
                ch.step(dve.tensor_reduce(total, wdense, AX.X, ALU.add))
                ch.step(dve.tensor_scalar(total, total, SUM_EPS, None, ALU.add))
                ch.step(dve.reciprocal(total, total))
                ch.step(dve.tensor_tensor(wdense, wdense, total.unsqueeze(2).broadcast_to([P, NT, E]), ALU.mult))
                ch.step(dve.tensor_scalar(wdense, wdense, RSF, None, ALU.mult))
                dve.sem_inc(w_ready, 1)

                def hidden(slot, row_q, weights):
                    for g in range(NTH):
                        dve.wait_ge(h_psum, row_q * 2 + (g + 1))
                        if weights is None:
                            a = dve.tensor_scalar(relu_w[:, g, :], psum[:, g, :], 0.0, None, ALU.max)
                        else:
                            if g == 0:
                                dve.wait_ge(gw_loaded[slot], weights)
                            a = dve.scalar_tensor_tensor(out=relu_w[:, g, :], in0=psum[:, g, :], scalar=0.0,
                                                         in1=gw_ring[:, slot, g * TH:(g + 1) * TH],
                                                         op0=ALU.max, op1=ALU.mult)
                        a.then_inc(weighted, 1)
                    if weights is not None:
                        dve.wait_ge(chunk_used, row_q + (FREE - 1))
                    for g in range(NTH):
                        dve.wait_ge(weighted, row_q * 2 + (g + 1))
                        dve.scalar_tensor_tensor(out=hid[:, slot % 2, g, :], in0=psum[:, g, :], scalar=0.0,
                                                 in1=relu_w[:, g, :], op0=ALU.max, op1=ALU.mult).then_inc(hid_ready, 1)

                hidden(0, b * NQ, None)
                hidden(1, b * NQ + 1, None)
                dve.wait_ge(wT_psum, b + 1)
                dve.tensor_copy(wT_sb, psum[0:E, 2:4, :].rearrange("p a t -> p (a t)")).then_inc(wT_copied, 1)
                with dve.Fori(0, NCH // UNROLL) as i:
                    for j in range(UNROLL):
                        q = b * NQ + i * UNROLL + (NSH + j)
                        hidden(j, q, b * (NCH // UNROLL * 32) + i * 32 + 32)

                dve.wait_ge(chunk_used, b * NQ + (NQ + FREE))
                for h in range(2):
                    for i in range(h * NT // 2, (h + 1) * NT // 2):
                        ch.step(dve.tensor_tensor(gated_y[:, i % 2, :], psum[:, 4 + i // 2, (i % 2) * C:(i % 2 + 1) * C],
                                                  modrow[:, 1, bass.ds(b, 1), :].squeeze(1), ALU.mult))
                        ch.add(dve.tensor_tensor(xrow(i), xrow(i), gated_y[:, i % 2, :], ALU.add))
                    ch.settle()
                    dve.sem_inc(row_done, 1)
                assert ch.n == DVE_ROW




def _rotary_tables():
    fraction = np.arange(0, HD, 2, dtype=np.float32) / np.float32(HD)
    timescale = np.float32(10000.0) ** fraction
    angle = np.arange(T, dtype=np.float32)[:, None] * (np.float32(1.0) / timescale)[None, :]
    return np.cos(angle).astype(np.float32), np.sin(angle).astype(np.float32)


def kernel(L0_attn_x, L0_attn_Wq, L0_attn_Wk, L0_attn_Wv, L0_attn_Wout, L0_ffn_gate_w, L0_ffn_gate_bias,
           L0_ffn_w1, L0_ffn_w2, L0_ffn_shared_up, L0_ffn_shared_down, L0_c, L0_wmod):
    import concourse.bacc as bacc
    from concourse.bass_utils import run_bass_kernel_spmd

    cos, sin = _rotary_tables()
    arrays = {
        "x": np.asarray(L0_attn_x).reshape(B * T, C),
        "cT": np.asarray(L0_c).T,
        "wmod": L0_wmod,
        "wq": L0_attn_Wq, "wk": L0_attn_Wk, "wv": L0_attn_Wv, "wout": L0_attn_Wout,
        "gate_w": np.asarray(L0_ffn_gate_w).T,
        "gate_bias": L0_ffn_gate_bias,
        "w1": np.asarray(L0_ffn_w1).reshape(E * EI, C).T,
        "w2": np.asarray(L0_ffn_w2).transpose(0, 2, 1).reshape(E * EI, C),
        "up": np.asarray(L0_ffn_shared_up).T,
        "down": np.asarray(L0_ffn_shared_down).T,
        "cos": cos, "sin": sin,
        "eye": np.eye(P, dtype=np.float32),
        "before": np.tril(np.ones((NG, NG), np.float32), -1),
    }
    arrays = {f"in_{k}": np.ascontiguousarray(v) for k, v in arrays.items()}
    nc = bacc.Bacc("TRN2", target_bir_lowering=False, num_devices=1)
    args = [nc.dram_tensor(k, v.shape, mybir.dt.from_np(v.dtype), kind="ExternalInput").ap()
            for k, v in arrays.items()]
    args.append(nc.dram_tensor("out", (B * T, C), F32, kind="ExternalOutput").ap())
    adaln_layer(nc, *args)
    r = run_bass_kernel_spmd(nc, [arrays], core_ids=[0])
    return r.results[0]["out"].reshape(B, T, C)
```

```python
from contextlib import ExitStack

import numpy as np

import concourse.bass as bass
from concourse import mybir

F32 = mybir.dt.float32
BF16 = mybir.dt.bfloat16
F32R = mybir.dt.float32r
ALU = mybir.AluOpType
ACT = mybir.ActivationFunctionType
AX = mybir.AxisListType

P = 128
B, T, C = 4, 1024, 256
NT = T // P
CK = C // P
NH, NKV, HD = 16, 4, 16
G = NH // NKV
NQK = NH + NKV
QKV = (NH + 2 * NKV) * HD
HALF = HD // 2
PARTS = 6
KS = PARTS * HD
E, NG, TOPG, TOPK = 64, 8, 4, 6
EG = E // NG
EI = 64
SH = 256
RSF = 2.5
TH = 512
NTH = T // TH
TPH = TH // P
NSH = SH // P
NCH = E * EI // P
NQ = NSH + NCH
RING = 4
UNROLL = RING
FREE = 2
MODS = (0, 1, 3, 4)
TURNS = NCH // UNROLL
assert TURNS == NT
STEPS = NTH * NKV * NT
MASKED, SENTINEL, CHOSEN = -3.0e38, -3.2e38, 3.0e38
LN_EPS, RMS_EPS, SUM_EPS = 1e-5, 1e-6, 1e-20


def hold(eng, held, sem, value):
    eng.wait_ge(sem, value)
    eng.sem_inc(held, 1)


class Chain:

    def __init__(self, eng, sem, held, base=0, row=None, per=0):
        self.eng, self.sem, self.held, self.base, self.row, self.per = eng, sem, held, base, row, per
        self.n = 0

    def add(self, ins):
        ins.then_inc(self.sem, 1)
        self.n += 1

    def settle(self, apart=False):
        k = self.base + self.n
        if self.row is not None:
            k = self.row * self.per + k
        if apart:
            hold(self.eng, self.held, self.sem, k)
        else:
            self.eng.wait_ge(self.sem, k)

    def step(self, ins, apart=False):
        self.add(ins)
        self.settle(apart)


DVE_ROW = 102
POOL_ROW = 1
DVE_TILE = 13
POOL_TILE = 5
PASSES = ((0, 0), (0, 1), (1, 0))


def tile_of(per, n, k=0):
    return n * per + (per + k)


def half_of(q, g):
    return q * NTH + (g + 1 + NTH)


def half_before(q, g):
    return q * NTH + (g + 1)


def adaln_layer(nc, x, cT, wmod, wq, wk, wv, wout, gate_w, gate_bias, w1, w2, up, down, cos, sin,
                eye, before, out):
    wT = nc.dram_tensor("gate_weights_T", [E, T], F32, kind="Internal").ap()

    with ExitStack() as ctx:
        def sb(name, shape, dt=F32):
            return ctx.enter_context(nc.sbuf_tensor(name, shape, dt))

        def sb_under(name, shape, dt=F32):
            with nc.sbuf_tensor(name, shape, dt) as t:
                return t

        def sem(name):
            return ctx.enter_context(nc.semaphore(name))

        psum = ctx.enter_context(nc.psum_tensor("psum", [P, 8, 512], F32))

        ident = sb("ident", [P, P])
        ident_b = sb("ident_b", [P, P], BF16)
        cos_sb, sin_sb = sb("cos_sb", [P, NT, HALF]), sb("sin_sb", [P, NT, HALF])
        before_sb = sb("before_sb", [P, NG, NG])
        bias_sb = sb("bias_sb", [P, E])
        wqkv_parts = sb("wqkv_parts", [P, 2, CK, QKV], F32R)
        wout_sb = sb("wout_sb", [P, NKV, C])
        gate_parts = sb("gate_parts", [P, 2, CK, E], F32R)
        minus_half = sb("minus_half", [P, NT])
        c_sb = sb("c_sb", [P, CK, B])
        silu = sb("silu", [P, CK, B])
        modcol = sb("modcol", [P, len(MODS) * CK, B])
        modrow = sb("modrow", [P, 2, B, C])
        xs = sb("xs", [P, B * NT, C])
        stats1 = sb("stats1", [P, 6])
        mv1 = sb("mv1", [P, 2])
        rstd1 = sb("rstd1", [P, 1])
        curmod1 = sb("curmod1", [P, 2 * CK])
        xn1 = sb("xn1", [P, C])
        h1_full = sb("h1_full", [P, CK, P])
        h1_parts = sb("h1_parts", [P, 2, CK, P], F32R)
        ssq = sb("ssq", [P, 2])
        rrms = sb("rrms", [P, 2])
        qk = sb("qk", [P, NQK * HD])
        rope = [sb(f"rope{i}", [P, NQK, HALF]) for i in range(4)]
        rot = sb("rot", [P, NQK, HD])
        rest = sb("rest", [P, NQK, HD])
        stack = sb("stack", [P, NQK, PARTS, HD], BF16)
        QT = sb("QT", [KS, NH, T], BF16)
        KT = sb("KT", [KS, NKV, T], BF16)
        V1 = sb("V1", [P, NT, NKV, 2 * HD])
        probs = sb("probs", [P, 3, G, TH])
        o_sb = sb_under("o_sb", [P, 2, TH])
        w1_parts = sb("w1_parts", [P, 2, 2, CK, P], F32R)
        o_den = sb("o_den", [P, TH])
        encT = sb_under("encT", [P, NKV, T])
        hid_parts = sb("hid_parts", [P, 2, 2, T], F32R)
        gated_y = sb("gated_y", [P, 2, C])
        stats2 = sb("stats2", [P, NT, 6])
        mv2 = sb("mv2", [P, NT, 2])
        rstd2 = sb("rstd2", [P, NT])
        curmod2 = sb("curmod2", [P, 2 * CK])
        xn = sb_under("xn", [P, NT, C])
        relu_w = sb("relu_w", [P, NTH, TH])
        w2_parts = sb("w2_parts", [P, 2, 2, C], F32R)
        h_full = sb("h_full", [P, 2, CK, P])
        hT_parts = sb("hT_parts", [P, 2, CK, T], F32R)
        VW = E + 2
        cand = sb("cand", [P, NT, VW])
        wdense = sb("wdense", [P, NT, E])
        tmp_all = sb("tmp_all", [P, 4, 576])
        tmp = [tmp_all[:, i, :] for i in range(4)]
        w1_ring = sb("w1_ring", [P, RING, CK, P])
        w2_ring = sb("w2_ring", [P, RING, C])
        flat = probs[:, :, :, :].rearrange("p a g t -> p (a g t)")
        enc_flat = encT[:, :, :].rearrange("p k t -> p (k t)")
        wmod_sb = flat[:, 0:CK * 6 * C].rearrange("p (k n) -> p k n", k=CK)
        siluB = flat[:, CK * 6 * C:CK * 6 * C + CK * B * P].rearrange("p (k b n) -> p k b n", k=CK, b=B)
        rowtmp = enc_flat[:, 0:2 * B * C]
        wqkv_full = enc_flat[:, 2 * B * C:2 * B * C + CK * QKV].rearrange("p (k n) -> p k n", k=CK)
        gate_full = enc_flat[:, 2 * B * C + CK * QKV:2 * B * C + CK * (QKV + E)].rearrange("p (k n) -> p k n", k=CK)
        gw_ring = flat[:, 0:RING * T].rearrange("p (s t) -> p s t", s=RING)
        relued = flat[:, RING * T:(RING + 1) * T].rearrange("p (g t) -> p g t", g=NTH)
        hid_full = flat[:, (RING + 1) * T:(RING + 2) * T].rearrange("p (g t) -> p g t", g=NTH)
        scores = enc_flat[:, 0:NT * E]
        sbias = enc_flat[:, NT * E:2 * NT * E]
        squares = o_den
        wT_sb = tmp_all[:, :, :].rearrange("p a t -> p (a t)")[0:E, 0:T]

        x_loaded = sem("x_loaded")
        w_loaded = sem("w_loaded")
        wmod_loaded = sem("wmod_loaded")
        zeros_set = sem("zeros_set")
        dve_chain = sem("dve_chain")
        tile_chain = sem("tile_chain")
        stat_chain = sem("stat_chain")
        pool_chain = sem("pool_chain")
        pool_tile_chain = sem("pool_tile_chain")
        pool_stat_chain = sem("pool_stat_chain")
        held = sem("held")
        held_pool = sem("held_pool")
        held_sp = sem("held_sp")
        held_pe = sem("held_pe")
        consts_set = sem("consts_set")
        silu_exp = sem("silu_exp")
        silu_ready = sem("silu_ready")
        mod_cols = sem("mod_cols")
        mod_rows = sem("mod_rows")
        mod_done = sem("mod_done")
        mods_set = sem("mods_set")
        p_stats = sem("p_stats")
        p_rstd = sem("p_rstd")
        p_xn = sem("p_xn")
        p_xnT = sem("p_xnT")
        p_mod = sem("p_mod")
        p_h = sem("p_h")
        p_qkv = sem("p_qkv")
        p_squares = sem("p_squares")
        p_v = sem("p_v")
        p_rrms = sem("p_rrms")
        p_parts = sem("p_parts")
        p_qrep = sem("p_qrep")
        p_krep = sem("p_krep")
        p_stackT = sem("p_stackT")
        p_copied = sem("p_copied")
        logits_ready = sem("logits_ready")
        exp_done = sem("exp_done")
        pv_done = sem("pv_done")
        o_copied = sem("o_copied")
        enc_ready = sem("enc_ready")
        y_psum = sem("y_psum")
        y_read = sem("y_read")
        stats_ready = sem("stats_ready")
        rstd_ready = sem("rstd_ready")
        xn_ready = sem("xn_ready")
        xnT_ready = sem("xnT_ready")
        h_modulated = sem("h_modulated")
        hT_ready = sem("hT_ready")
        logit_psum = sem("logit_psum")
        escore = sem("escore")
        w_ready = sem("w_ready")
        wT_psum = sem("wT_psum")
        wT_copied = sem("wT_copied")
        wT_stored = sem("wT_stored")
        chunk_loaded = [sem(f"chunk_loaded{s}") for s in range(RING)]
        gw_loaded = [sem(f"gw_loaded{s}") for s in range(RING)]
        w1_hi = sem("w1_hi")
        w1_lo = sem("w1_lo")
        w2_hi = sem("w2_hi")
        w2_lo = sem("w2_lo")
        h_psum = sem("h_psum")
        h_relued = sem("h_relued")
        hid_ready = sem("hid_ready")
        hid_hi = sem("hid_hi")
        hid_lo = sem("hid_lo")
        weighted = sem("weighted")
        chunk_used = sem("chunk_used")
        bank_read = sem("bank_read")
        row_done = sem("row_done")
        stored = sem("stored")

        block = ctx.enter_context(nc.Block())

        def rows(eng, row):
            with eng.Fori(0, B - 1) as b:
                row(b, True)
            row(B - 1, False)

        def loads_before(b, i, slot):
            return b * TURNS + i if slot < 2 else b * (TURNS + 1) + i + 1

        @block.sync
        def _(sp):
            sp.dma_start(c_sb[:, :, :], cT.rearrange("(k p) b -> p k b", p=P)).then_inc(wmod_loaded, 16)
            sp.dma_start(wmod_sb, wmod.rearrange("(k p) n -> p k n", p=P)).then_inc(wmod_loaded, 16)
            sp.dma_start(xs[:, 0:NT, :], x[0:T, :].rearrange("(t p) c -> p t c", p=P)).then_inc(x_loaded, 16)
            sp.dma_start(ident[:, :], eye).then_inc(w_loaded, 16)
            sp.dma_start(wqkv_full[:, :, 0:C], wq.rearrange("(k p) n -> p k n", p=P)).then_inc(w_loaded, 16)
            sp.dma_start(wqkv_full[:, :, C:C + 64], wk.rearrange("(k p) n -> p k n", p=P)).then_inc(w_loaded, 16)
            sp.dma_start(wqkv_full[:, :, C + 64:QKV], wv.rearrange("(k p) n -> p k n", p=P)).then_inc(w_loaded, 16)
            sp.dma_start(gate_full, gate_w.rearrange("(k p) e -> p k e", p=P)).then_inc(w_loaded, 16)
            sp.dma_start(cos_sb[:, :, :], cos.rearrange("(t p) f -> p t f", p=P)).then_inc(w_loaded, 16)
            sp.dma_start(sin_sb[:, :, :], sin.rearrange("(t p) f -> p t f", p=P)).then_inc(w_loaded, 16)
            sp.dma_start(before_sb[:, :, :], before.unsqueeze(0).broadcast_to([P, NG, NG])).then_inc(w_loaded, 16)
            sp.dma_start(bias_sb[:, :], gate_bias.unsqueeze(0).broadcast_to([P, E])).then_inc(w_loaded, 16)
            sp.wait_ge(zeros_set, 1)
            wo = wout.rearrange("(k g h) c -> g h k c", k=NKV, g=G)
            for g in range(G):
                sp.dma_start(wout_sb[32 * g:32 * g + HD, :, :], wo[g]).then_inc(w_loaded, 16)
            sp.dma_start(xs[:, NT:B * NT, :], x[T:B * T, :].rearrange("(t p) c -> p t c", p=P)).then_inc(x_loaded, 16)

            def row(b, more):
                hold(sp, held_sp, w2_lo, b * NQ + FREE)
                for q in range(NSH):
                    sp.dma_start(w1_ring[:, q + 2, :, :],
                                 up[:, q * P:(q + 1) * P].rearrange("(k p) n -> p k n", p=P)
                                 ).then_inc(chunk_loaded[q + 2], 16)
                    sp.dma_start(w2_ring[:, q + 2, :], down[q * P:(q + 1) * P, :]).then_inc(chunk_loaded[q + 2], 16)
                hold(sp, held_sp, wT_copied, b + 1)
                sp.dma_start(wT, wT_sb).then_inc(wT_stored, 16)
                hold(sp, held_sp, wT_stored, b * 16 + 16)
                with sp.Fori(0, TURNS) as i:
                    for j in range(UNROLL):
                        hold(sp, held_sp, w2_lo, b * NQ + i * UNROLL + (NSH + j - RING + 1 + FREE))
                        hold(sp, held_sp, weighted, b * (2 * NCH) + i * (2 * UNROLL) + (2 * j + 2))
                        for k in range(2):
                            src = wT[bass.ds(i * 2 * UNROLL + (2 * j + k), 1), :].broadcast_to([EI, T])
                            sp.dma_start(gw_ring[EI * k:EI * k + EI, j, :], src).then_inc(gw_loaded[j], 16)
                        sp.dma_start(w1_ring[:, j, :, :],
                                     w1[:, bass.ds(i * UNROLL * P + j * P, P)].rearrange("(k p) n -> p k n", p=P)
                                     ).then_inc(chunk_loaded[j], 16)
                        sp.dma_start(w2_ring[:, j, :], w2[bass.ds(i * UNROLL * P + j * P, P), :]
                                     ).then_inc(chunk_loaded[j], 16)
                for h in range(2):
                    hold(sp, held_sp, row_done, b * 2 + (h + 1))
                    n = NT // 2
                    sp.dma_start(out[bass.ds(b * T + h * (T // 2), T // 2), :].rearrange("(t p) c -> p t c", p=P),
                                 xs[:, bass.ds(b * NT + h * n, n), :]).then_inc(stored, 16)

            rows(sp, row)
            hold(sp, held_sp, stored, B * 32)

        @block.tensor
        def _(pe):
            def psum_b(k):
                return psum[:, k, :].bitcast(BF16)

            pe.wait_ge(wmod_loaded, 32)
            pe.wait_ge(silu_ready, 1)
            for m, mod in enumerate(MODS):
                for k in range(CK):
                    o = psum[:, 0, (m * CK + k) * B:(m * CK + k + 1) * B]
                    for c in range(CK):
                        mm = pe.matmul(o, wmod_sb[:, c, mod * C + k * P:mod * C + (k + 1) * P], silu[:, c, :],
                                       start=(c == 0), stop=(c == CK - 1))
            mm.then_inc(mod_cols, 1)
            for r, mod in enumerate((2, 5)):
                for b in range(B):
                    o = psum[:, 1 + r * 2 + b // 2, (b % 2) * C:(b % 2 + 1) * C]
                    for c in range(CK):
                        mm = pe.matmul(o, siluB[:, c, b, :], wmod_sb[:, c, mod * C:(mod + 1) * C],
                                       start=(c == 0), stop=(c == CK - 1))
            mm.then_inc(mod_rows, 1)
            pe.wait_ge(w_loaded, 16 * 13)
            pe.wait_ge(consts_set, 1)
            pe.wait_ge(mod_done, 1)
            pe.sem_inc(chunk_used, FREE)
            pe.sem_inc(h_psum, NTH)
            pe.sem_inc(p_xnT, 1)
            pe.sem_inc(p_qkv, 1)
            pe.sem_inc(p_stackT, 3)

            def transpose_x(n):
                pe.wait_ge(p_xn, tile_of(1, n, 1))
                pe.wait_ge(p_mod, tile_of(1, n))
                for k in range(CK):
                    mm = pe.transpose(psum[:, 2, k * P:(k + 1) * P], xn1[:, k * P:(k + 1) * P], ident[:, :])
                mm.then_inc(p_xnT, 1)

            def project(n):
                pe.wait_ge(p_h, tile_of(1, n, 1))
                pe.wait_ge(p_copied, tile_of(3, n))
                for k in range(CK):
                    for a, c in PASSES:
                        mm = pe.matmul(psum[:, 3, 0:QKV], h1_parts[:, a, k, :], wqkv_parts[:, c, k, :],
                                       start=(k == 0 and (a, c) == PASSES[0]),
                                       stop=(k == CK - 1 and (a, c) == PASSES[-1]))
                mm.then_inc(p_qkv, 1)

            def transpose_stack(bank, heads):
                for i, h in enumerate(heads):
                    mm = pe.transpose(psum_b(bank)[0:KS, i * P:(i + 1) * P],
                                      stack[:, h, :, :].rearrange("p a d -> p (a d)"), ident_b[:, :])
                mm.then_inc(p_stackT, 1)

            def transpose_low(n):
                pe.wait_ge(p_parts, tile_of(1, n, 1))
                pe.wait_ge(p_qrep, tile_of(1, n, 1))
                transpose_stack(3, range(0, 8))

            def transpose_high(n, more):
                pe.wait_ge(p_copied, tile_of(3, n, 1))
                transpose_stack(3, range(8, NH))
                pe.wait_ge(p_krep, tile_of(1, n, 1))
                if more:
                    pe.wait_ge(p_mod, tile_of(1, n + 1, 1))
                transpose_stack(2, range(NH, NQK))

            transpose_x(0)
            with pe.Fori(0, NT - 1) as i:
                project(i)
                transpose_x(i + 1)
                transpose_low(i)
                transpose_high(i, True)
            project(NT - 1)
            transpose_low(NT - 1)
            transpose_high(NT - 1, False)

            def row(b, more):
                def logits(st, pair):
                    th, kv, s = st // (NKV * NT), st // NT % NKV, st % NT
                    n = 2 * st + pair
                    if n == 2:
                        pe.wait_ge(bank_read, b * (NT // 2) + 2)
                    if n >= 3:
                        pe.wait_ge(exp_done, b * 2 * STEPS + (n - 2))
                    for k in range(2):
                        mm = pe.matmul(psum[:, 2 * (n % 3) + k, :], KT[:, kv, s * P:(s + 1) * P],
                                       QT[:, kv * G + 2 * pair + k, th * TH:(th + 1) * TH], start=True, stop=True)
                    mm.then_inc(logits_ready, 1)

                def attend(st):
                    kv, s = st // NT % NKV, st % NT
                    if st == 0:
                        pe.wait_ge(bank_read, b * (NT // 2) + 3)
                    pe.wait_ge(exp_done, b * 2 * STEPS + (2 * st + 2))
                    if s == 0 and st >= NT:
                        pe.wait_ge(o_copied, b * NTH * NKV + st // NT)
                    for g in range(G):
                        mm = pe.matmul(psum[32 * g:32 * g + 32, 6, :], V1[:, s, kv, :], probs[:, st % 3, g, :],
                                       start=(s == 0), stop=(s == NT - 1))
                    mm.then_inc(pv_done, 1)

                def project_out(i):
                    pe.wait_ge(enc_ready, b * NTH * NKV + (i // TPH + 1) * NKV)
                    if i == 0:
                        pe.wait_ge(bank_read, b * (NT // 2) + 4)
                    if i >= 1:
                        pe.wait_ge(y_read, b * NT + i)
                    for kv in range(NKV):
                        mm = pe.matmul(psum[:, 7, (i % 2) * C:(i % 2 + 1) * C], encT[:, kv, i * P:(i + 1) * P],
                                       wout_sb[:, kv, :], start=(kv == 0), stop=(kv == NKV - 1))
                    mm.then_inc(y_psum, 1)

                pe.wait_ge(p_copied, tile_of(3, b * NT + (NT - 1), 3))
                pe.wait_ge(p_v, tile_of(1, b * NT + (NT - 1), 1))
                for st in range(STEPS + 1):
                    if st < STEPS:
                        logits(st, 0)
                        logits(st, 1)
                    if st >= 1:
                        attend(st - 1)
                    r = st - NKV * NT - 3
                    if r >= 0 and r < TPH:
                        project_out(r)
                for i in range(TPH, NT):
                    project_out(i)

                for i in range(NT):
                    pe.wait_ge(xn_ready, b * NT + (i + 1))
                    if i >= 2:
                        pe.wait_ge(h_modulated, b * NT + (i - 1))
                    for k in range(CK):
                        mm = pe.transpose(psum[:, i % 2, k * P:(k + 1) * P], xn[:, i, k * P:(k + 1) * P], ident[:, :])
                    mm.then_inc(xnT_ready, 1)
                for i in range(NT):
                    pe.wait_ge(hT_ready, b * NT + (i + 1))
                    for k in range(CK):
                        for a, c in PASSES:
                            mm = pe.matmul(psum[:, 2, i * E:(i + 1) * E], hT_parts[:, a, k, i * P:(i + 1) * P],
                                           gate_parts[:, c, k, :],
                                           start=(k == 0 and (a, c) == PASSES[0]),
                                           stop=(k == CK - 1 and (a, c) == PASSES[-1]))
                mm.then_inc(logit_psum, 1)

                def up_chunk(hslot, q):
                    for g in range(NTH):
                        pe.wait_ge(h_relued, half_before(q, g))
                        if g == 0:
                            pe.wait_ge(w1_lo, q + 1)
                        for k in range(CK):
                            for a, c in PASSES:
                                mm = pe.matmul(psum[:, g, :], w1_parts[:, a, hslot, k, :],
                                               hT_parts[:, c, k, g * TH:(g + 1) * TH],
                                               start=(k == 0 and (a, c) == PASSES[0]),
                                               stop=(k == CK - 1 and (a, c) == PASSES[-1]))
                        mm.then_inc(h_psum, 1)

                def down_chunk(hslot, q, first=False):
                    for i in range(NT):
                        if i == 0:
                            pe.wait_ge(w2_lo, q + (1 + FREE))
                        if i % TPH == 0:
                            pe.wait_ge(hid_lo, half_of(q, i // TPH))
                        for a, c in PASSES:
                            mm = pe.matmul(psum[:, 4 + i // 2, (i % 2) * C:(i % 2 + 1) * C],
                                           hid_parts[:, a, hslot, i * P:(i + 1) * P], w2_parts[:, c, hslot, :],
                                           start=(first and i % 2 == 0 and (a, c) == PASSES[0]), stop=True,
                                           skip_group_check=True)
                    mm.then_inc(chunk_used, 1)

                up_chunk(0, b * NQ)
                nxt = b * NT + NT
                if more:
                    pe.wait_ge(escore, b + 1)
                    transpose_x(nxt)
                up_chunk(1, b * NQ + 1)
                hold(pe, held_pe, w_ready, b + 1)
                if more:
                    hold(pe, held_pe, p_mod, tile_of(1, nxt, 1))
                for i in range(NT):
                    mm = pe.transpose(psum[0:E, 2 + i // TPH, (i % TPH) * P:(i % TPH + 1) * P],
                                      wdense[:, i, :], ident[:, :])
                mm.then_inc(wT_psum, 1)
                down_chunk(0, b * NQ, True)
                hold(pe, held_pe, wT_copied, b + 1)

                def turn(i, second, first):
                    q = b * NQ + i * UNROLL + NSH
                    n = nxt + i
                    up_chunk(0, q)
                    if second:
                        project(n)
                    down_chunk(1, q - 1)
                    up_chunk(1, q + 1)
                    down_chunk(0, q)
                    up_chunk(0, q + 2)
                    down_chunk(1, q + 1)
                    up_chunk(1, q + 3)
                    if first:
                        transpose_x(n + 1)
                    if second:
                        transpose_low(n)
                    down_chunk(0, q + 2)
                    if second:
                        transpose_high(n, first)

                with pe.Fori(0, TURNS - 1) as i:
                    turn(i, more, more)
                turn(TURNS - 1, more, False)
                down_chunk(1, b * NQ + (NQ - 1))

            rows(pe, row)

        @block.scalar
        def _(act):
            act.wait_ge(wmod_loaded, 32)
            act.activation(silu[:, :, :], c_sb[:, :, :], ACT.Exp, scale=-1.0).then_inc(silu_exp, 1)
            act.sem_inc(p_mod, 1)
            act.sem_inc(p_squares, 2)
            act.sem_inc(p_v, 1)
            act.sem_inc(p_qrep, 1)
            act.sem_inc(p_copied, 3)
            act.sem_inc(h_relued, NTH)
            act.sem_inc(hid_hi, NTH)

            def modulate(full, hi, bank, mods, k):
                a = None
                for o in (full, hi):
                    a = act.activation(o, psum[:, bank, k * P:(k + 1) * P], ACT.Identity,
                                       bias=mods[:, k:k + 1], scale=mods[:, k + CK:k + CK + 1])
                return a

            def modulate_tile(n):
                act.wait_ge(p_xnT, tile_of(1, n, 1))
                act.wait_ge(p_qkv, tile_of(1, n))
                for k in range(CK):
                    a = modulate(h1_full[:, k, :], h1_parts[:, 0, k, :], 2, curmod1, k)
                a.then_inc(p_mod, 1)

            def square(n, i):
                act.wait_ge(p_qkv, tile_of(1, n, 1))
                act.activation(V1[:, bass.ds(i, 1), :, 0:HD].squeeze(1),
                               psum[:, 3, NQK * HD:QKV].rearrange("p (k d) -> p k d", k=NKV),
                               ACT.Copy).then_inc(p_v, 1)
                act.wait_ge(p_squares, tile_of(2, n))
                act.activation(squares[:, 0:NH * HD], psum[:, 3, 0:NH * HD], ACT.Square,
                               accum_out=ssq[:, 0:1]).then_inc(p_squares, 1)
                act.activation(squares[:, NH * HD:NQK * HD], psum[:, 3, NH * HD:NQK * HD], ACT.Square,
                               accum_out=ssq[:, 1:2]).then_inc(p_squares, 1)

            def replicate(n):
                act.wait_ge(p_parts, tile_of(1, n, 1))
                for src, dst in ((0, 1), (0, 3), (5, 2)):
                    a = act.activation(stack[:, 0:NH, dst, :], stack[:, 0:NH, src, :], ACT.Copy)
                a.then_inc(p_qrep, 1)

            def copy_stack(n, k, dst, bank):
                act.wait_ge(p_stackT, tile_of(3, n, k))
                h = dst.shape[1]
                act.activation(dst, psum[:, bank, :].bitcast(BF16)[0:KS, 0:h * P].rearrange("p (h t) -> p h t", h=h),
                               ACT.Copy).then_inc(p_copied, 1)

            def copy_low(n, i):
                copy_stack(n, 1, QT[:, 0:8, bass.ds(i * P, P)], 3)

            def copy_high(n, i):
                copy_stack(n, 2, QT[:, 8:16, bass.ds(i * P, P)], 3)
                copy_stack(n, 3, KT[:, :, bass.ds(i * P, P)], 2)

            modulate_tile(0)
            with act.Fori(0, NT - 1) as i:
                square(i, i)
                modulate_tile(i + 1)
                replicate(i)
                copy_low(i, i)
                copy_high(i, i)
            square(NT - 1, NT - 1)
            replicate(NT - 1)
            copy_low(NT - 1, NT - 1)
            copy_high(NT - 1, NT - 1)

            def row(b, more):
                for st in range(STEPS):
                    for pair in range(2):
                        n = 2 * st + pair
                        act.wait_ge(logits_ready, b * 2 * STEPS + (n + 1))
                        if st >= 3 and pair == 0:
                            act.wait_ge(pv_done, b * STEPS + (st - 2))
                        act.activation(probs[:, st % 3, 2 * pair:2 * pair + 2, :], psum[:, 2 * (n % 3):2 * (n % 3) + 2, :],
                                       ACT.Exp).then_inc(exp_done, 1)
                for i in range(NT):
                    act.wait_ge(xnT_ready, b * NT + (i + 1))
                    if i == 0:
                        act.wait_ge(stats_ready, b + 1)
                    if i >= 2:
                        act.wait_ge(hT_ready, b * NT + (i - 1))
                    for k in range(CK):
                        a = modulate(h_full[:, i % 2, k, :], hT_parts[:, 0, k, i * P:(i + 1) * P], i % 2, curmod2, k)
                    a.then_inc(h_modulated, 1)

                def split_w1(hslot, slot, q, loads, first=False):
                    act.wait_ge(chunk_loaded[slot], loads * 32 + 32)
                    if not first:
                        act.wait_ge(h_psum, q * 2)
                    act.activation(w1_parts[:, 0, hslot, :, :], w1_ring[:, slot, :, :], ACT.Copy).then_inc(w1_hi, 1)

                def split_w2(hslot, slot, q, loads):
                    act.wait_ge(chunk_loaded[slot], loads * 32 + 32)
                    act.wait_ge(chunk_used, q + (FREE - 1))
                    act.activation(w2_parts[:, 0, hslot, :], w2_ring[:, slot, :], ACT.Copy).then_inc(w2_hi, 1)

                def relu(q):
                    for g in range(NTH):
                        act.wait_ge(h_psum, half_of(q, g))
                        act.wait_ge(hid_ready, half_before(q, g))
                        act.activation(relued[:, g, :], psum[:, g, :], ACT.Relu).then_inc(h_relued, 1)

                def split_hid(hslot, q):
                    for g in range(NTH):
                        act.wait_ge(hid_ready, half_of(q, g))
                        if g == 0:
                            act.wait_ge(chunk_used, q + (FREE - 1))
                        act.activation(hid_parts[:, 0, hslot, g * TH:(g + 1) * TH], hid_full[:, g, :],
                                       ACT.Copy).then_inc(hid_hi, 1)

                shared = b * (TURNS + 1)
                split_w1(0, 2, b * NQ, shared, True)
                act.wait_ge(logit_psum, b + 1)
                act.activation(scores, psum[:, 2, :], ACT.Exp, scale=-1.0).then_inc(escore, 1)
                nxt = b * NT + NT
                split_w1(1, 3, b * NQ + 1, shared, True)
                split_w2(0, 2, b * NQ, shared)
                relu(b * NQ)
                if more:
                    modulate_tile(nxt)
                split_w2(1, 3, b * NQ + 1, shared)
                split_hid(0, b * NQ)
                relu(b * NQ + 1)
                split_w1(0, 0, b * NQ + NSH, loads_before(b, 0, 0))
                split_hid(1, b * NQ + 1)

                def turn(i, second, first):
                    n = nxt + i
                    for j in range(UNROLL):
                        q = b * NQ + i * UNROLL + (NSH + j)
                        relu(q)
                        if j < UNROLL - 1:
                            split_w1((j + 1) % 2, j + 1, q + 1, loads_before(b, i, j + 1))
                        elif not (isinstance(i, int) and i == TURNS - 1):
                            split_w1(0, 0, q + 1, loads_before(b, i + 1, 0))
                        split_w2(j % 2, j, q, loads_before(b, i, j))
                        if second and j == 0:
                            square(n, i)
                        if j == UNROLL - 1:
                            if first:
                                modulate_tile(n + 1)
                            if second:
                                copy_low(n, i)
                        split_hid(j % 2, q)
                        if second and j == 2:
                            replicate(n)
                    if second:
                        copy_high(n, i)

                with act.Fori(0, TURNS - 1) as i:
                    turn(i, more, more)
                turn(TURNS - 1, more, False)

            rows(act, row)

        @block.gpsimd
        def _(pool):
            pool.memset(wout_sb[:, :, :], 0.0).then_inc(zeros_set, 1)
            pool.memset(V1[:, :, :, HD:2 * HD], 1.0)
            pool.memset(minus_half[:, :], -0.5).then_inc(consts_set, 1)
            pool.wait_ge(consts_set, 1)
            pool.sem_inc(p_rstd, 1)
            pool.sem_inc(p_h, 1)
            pool.sem_inc(p_rrms, 1)
            pool.sem_inc(p_krep, 1)
            pool.sem_inc(w2_lo, FREE)

            def rstd_tile(n):
                ch = Chain(pool, pool_stat_chain, held_pool, 0, n, 1)
                hold(pool, held_pool, p_stats, tile_of(1, n, 1))
                ch.step(pool.tensor_scalar(rstd1[:, :], mv1[:, 1:2], LN_EPS, None, ALU.add))
                pool.tensor_tensor(rstd1[:, :], rstd1[:, :], minus_half[:, 0:1], ALU.pow).then_inc(p_rstd, 1)

            def lo_tile(n):
                hold(pool, held_pool, p_mod, tile_of(1, n, 1))
                pool.tensor_tensor(h1_parts[:, 1, :, :], h1_full[:, :, :], h1_parts[:, 0, :, :],
                                   ALU.subtract).then_inc(p_h, 1)

            def rms_tile(n):
                ch = Chain(pool, pool_tile_chain, held_pool, 0, n, POOL_TILE)
                hold(pool, held_pool, p_squares, tile_of(2, n, 2))
                ch.add(pool.tensor_scalar(rrms[:, 0:1], ssq[:, 0:1], 1.0 / (NH * HD), RMS_EPS, ALU.mult, ALU.add))
                ch.step(pool.tensor_scalar(rrms[:, 1:2], ssq[:, 1:2], 1.0 / (NKV * HD), RMS_EPS, ALU.mult, ALU.add))
                ch.step(pool.tensor_tensor(rrms[:, :], rrms[:, :], minus_half[:, 0:2], ALU.pow), apart=True)
                pool.tensor_scalar(rrms[:, 0:1], rrms[:, 0:1], HD ** -0.5, None, ALU.mult).then_inc(p_rrms, 1)
                return ch.n

            def keys_tile(n):
                ch = Chain(pool, pool_tile_chain, held_pool, 3, n, POOL_TILE)
                hold(pool, held_pool, p_parts, tile_of(1, n, 1))
                for src, dst in ((0, 2), (0, 4)):
                    ch.add(pool.tensor_copy(stack[:, NH:NQK, dst, :], stack[:, NH:NQK, src, :]))
                ch.settle(apart=True)
                pool.tensor_copy(stack[:, NH:NQK, 1, :], stack[:, NH:NQK, 5, :]).then_inc(p_krep, 1)
                assert 3 + ch.n == POOL_TILE

            rstd_tile(0)
            lo_tile(0)
            with pool.Fori(0, NT - 1) as i:
                rms_tile(i)
                rstd_tile(i + 1)
                lo_tile(i + 1)
                keys_tile(i)
            rms_tile(NT - 1)
            keys_tile(NT - 1)

            def row(b, more):
                ch = Chain(pool, pool_chain, held_pool, 0, b, POOL_ROW)
                hold(pool, held_pool, stats_ready, b + 1)
                ch.step(pool.tensor_scalar(rstd2[:, :], mv2[:, :, 1], LN_EPS, None, ALU.add))
                pool.tensor_tensor(rstd2[:, :], rstd2[:, :], minus_half[:, 0:NT], ALU.pow).then_inc(rstd_ready, 1)
                assert ch.n == POOL_ROW

                def split_w1(hslot, slot, q):
                    hold(pool, held_pool, w1_hi, q + 1)
                    pool.tensor_tensor(w1_parts[:, 1, hslot, :, :], w1_ring[:, slot, :, :], w1_parts[:, 0, hslot, :, :],
                                       ALU.subtract).then_inc(w1_lo, 1)

                def split_w2(hslot, slot, q):
                    hold(pool, held_pool, w2_hi, q + 1)
                    pool.tensor_tensor(w2_parts[:, 1, hslot, :], w2_ring[:, slot, :], w2_parts[:, 0, hslot, :],
                                       ALU.subtract).then_inc(w2_lo, 1)

                nxt = b * NT + NT
                if more:
                    rstd_tile(nxt)
                split_w1(0, 2, b * NQ)
                split_w1(1, 3, b * NQ + 1)
                split_w2(0, 2, b * NQ)
                if more:
                    lo_tile(nxt)
                split_w2(1, 3, b * NQ + 1)
                split_w1(0, 0, b * NQ + NSH)

                def turn(i, second, first):
                    n = nxt + i
                    for j in range(UNROLL):
                        q = b * NQ + i * UNROLL + (NSH + j)
                        if j < UNROLL - 1 or not (isinstance(i, int) and i == TURNS - 1):
                            split_w1((j + 1) % 2, (j + 1) % RING, q + 1)
                        split_w2(j % 2, j, q)
                        if second and j == 0:
                            rms_tile(n)
                        if first and j == 1:
                            rstd_tile(n + 1)
                        if second and j == 2:
                            keys_tile(n)
                        if first and j == 3:
                            lo_tile(n + 1)

                with pool.Fori(0, TURNS - 1) as i:
                    turn(i, more, more)
                turn(TURNS - 1, more, False)

            rows(pool, row)

        @block.vector
        def _(dve):
            su = Chain(dve, dve_chain, held)
            dve.sem_inc(p_stats, 1)
            dve.sem_inc(p_xn, 1)
            dve.sem_inc(p_parts, 1)
            dve.sem_inc(hid_ready, NTH)
            dve.sem_inc(hid_lo, NTH)
            dve.sem_inc(weighted, 2 * RING)
            dve.sem_inc(bank_read, NT // 2)
            dve.wait_ge(silu_exp, 1)
            su.step(dve.tensor_scalar(silu[:, :, :], silu[:, :, :], 1.0, None, ALU.add))
            su.step(dve.reciprocal(silu[:, :, :], silu[:, :, :]))
            su.step(dve.tensor_tensor(silu[:, :, :], silu[:, :, :], c_sb[:, :, :], ALU.mult))
            su.add(dve.tensor_copy(siluB.rearrange("p k b n -> p (k b) n"),
                                   silu[:, :, :].rearrange("p k b -> p (k b)").unsqueeze(2).broadcast_to([P, CK * B, P])))
            su.settle()
            dve.sem_inc(silu_ready, 1)
            dve.wait_ge(w_loaded, 16 * 13)
            su.add(dve.tensor_copy(ident_b[:, :], ident[:, :]))
            su.add(dve.tensor_copy(wqkv_parts[:, 0, :, :], wqkv_full))
            su.step(dve.tensor_copy(gate_parts[:, 0, :, :], gate_full))
            su.add(dve.tensor_tensor(wqkv_parts[:, 1, :, :], wqkv_full, wqkv_parts[:, 0, :, :], ALU.subtract))
            su.add(dve.tensor_tensor(gate_parts[:, 1, :, :], gate_full, gate_parts[:, 0, :, :], ALU.subtract))
            dve.wait_ge(mod_cols, 1)
            su.step(dve.tensor_copy(modcol[:, :, :].rearrange("p m b -> p (m b)"), psum[:, 0, 0:len(MODS) * CK * B]))
            for m in (1, 3):
                v = modcol[:, m * CK:(m + 1) * CK, :]
                su.add(dve.tensor_scalar(v, v, 1.0, None, ALU.add))
            dve.wait_ge(mod_rows, 1)
            for r in range(2):
                row = modrow[:, r, :, :].rearrange("p b c -> p (b c)")
                half = rowtmp[:, r * B * C:(r + 1) * B * C]
                for a, n in ((0, half.shape[1] // 2), (1, half.shape[1] // 2)):
                    hs, rs = half[:, a * n:(a + 1) * n], row[:, a * n:(a + 1) * n]
                    g = psum[:, 1 + 2 * r + a, :]
                    su.step(dve.tensor_scalar(hs, g, 0.0, 2.0, ALU.is_ge, ALU.mult))
                    su.step(dve.tensor_scalar(hs, hs, -1.0, None, ALU.add))
                    su.step(dve.tensor_tensor(rs, hs, g, ALU.mult))
                    su.step(dve.scalar_tensor_tensor(out=rs, in0=rs, scalar=0.25, in1=hs, op0=ALU.max, op1=ALU.mult))
            dve_setup = su.n
            dve.sem_inc(mod_done, 1)

            def stats_tile(n, b=None):
                ch = Chain(dve, stat_chain, held, 0, n, 2)
                hold(dve, held, p_xn, tile_of(1, n))
                ch.add(dve.bn_stats(stats1[:, :], xs[:, bass.ds(n, 1), :].squeeze(1)))
                if b is not None:
                    hold(dve, held, p_mod, tile_of(1, n))
                    dve.tensor_copy(curmod1[:, :], modcol[:, 0:2 * CK, bass.ds(b, 1)].squeeze(2)).then_inc(mods_set, 1)
                ch.settle(apart=True)
                ch.step(dve.bn_aggr(mv1[:, :], stats1[:, :]))
                if b is not None:
                    dve.wait_ge(mods_set, b + 1)
                dve.sem_inc(p_stats, 1)

            def normalise_tile(n):
                dve.wait_ge(p_rstd, tile_of(1, n, 1))
                dve.wait_ge(p_xnT, tile_of(1, n))
                dve.tensor_scalar(xn1[:, :], xs[:, bass.ds(n, 1), :].squeeze(1), mv1[:, 0:1], rstd1[:, 0:1],
                                  ALU.subtract, ALU.mult).then_inc(p_xn, 1)

            def rotate_tile(n, i):
                ch = Chain(dve, tile_chain, held, 0, n, DVE_TILE)
                dve.wait_ge(p_rrms, tile_of(1, n, 1))
                ch.add(dve.tensor_scalar(qk[:, 0:NH * HD], psum[:, 3, 0:NH * HD], rrms[:, 0:1], None, ALU.mult))
                ch.step(dve.tensor_scalar(qk[:, NH * HD:NQK * HD], psum[:, 3, NH * HD:NQK * HD], rrms[:, 1:2], None,
                                          ALU.mult))
                v = qk[:, :].rearrange("p (h d) -> p h d", h=NQK)
                cs = cos_sb[:, bass.ds(i, 1), :].broadcast_to([P, NQK, HALF])
                sn = sin_sb[:, bass.ds(i, 1), :].broadcast_to([P, NQK, HALF])
                for r, (part, tab) in enumerate(((0, cs), (1, sn), (1, cs), (0, sn))):
                    ch.add(dve.tensor_tensor(rope[r][:, :, :], v[:, :, part * HALF:(part + 1) * HALF], tab, ALU.mult))
                return ch

            def split_tile(n):
                ch = Chain(dve, tile_chain, held, 6, n, DVE_TILE)
                ch.settle()
                ch.add(dve.tensor_tensor(rot[:, :, 0:HALF], rope[0][:, :, :], rope[1][:, :, :], ALU.subtract))
                ch.step(dve.tensor_tensor(rot[:, :, HALF:HD], rope[2][:, :, :], rope[3][:, :, :], ALU.add))
                dve.wait_ge(p_stackT, tile_of(3, n))
                ch.step(dve.tensor_copy(stack[:, :, 0, :], rot[:, :, :]))
                ch.step(dve.tensor_tensor(rest[:, :, :], rot[:, :, :], stack[:, :, 0, :], ALU.subtract))
                ch.step(dve.tensor_copy(stack[:, :, 5, :], rest[:, :, :]))
                ch.add(dve.tensor_tensor(stack[:, 0:NH, 4, :], rest[:, 0:NH, :], stack[:, 0:NH, 5, :], ALU.subtract))
                ch.step(dve.tensor_tensor(stack[:, NH:NQK, 3, :], rest[:, NH:NQK, :], stack[:, NH:NQK, 5, :],
                                          ALU.subtract))
                dve.sem_inc(p_parts, 1)
                assert 6 + ch.n == DVE_TILE

            dve.wait_ge(x_loaded, 32)
            stats_tile(0, 0)
            normalise_tile(0)
            with dve.Fori(0, NT - 1) as i:
                rotate_tile(i, i)
                stats_tile(i + 1)
                normalise_tile(i + 1)
                split_tile(i)
            rotate_tile(NT - 1, NT - 1)
            split_tile(NT - 1)

            def row(b, more):
                ch = Chain(dve, dve_chain, held, dve_setup, b, DVE_ROW)

                def xrow(i):
                    return xs[:, bass.ds(b * NT + i, 1), :].squeeze(1)

                def divide(u):
                    th, kv = u // NKV, u % NKV
                    dve.wait_ge(pv_done, b * STEPS + (u + 1) * NT)
                    dve.tensor_copy(o_sb[:, u % 2, :], psum[:, 6, :]).then_inc(o_copied, 1)
                    hold(dve, held, o_copied, b * NTH * NKV + (u + 1))
                    ch.step(dve.stream_shuffle(o_den[:, :], o_sb[:, u % 2, :], [HD] * 32))
                    ch.step(dve.reciprocal(o_den[:, :], o_den[:, :]))
                    dve.tensor_tensor(encT[:, kv, th * TH:(th + 1) * TH], o_sb[:, u % 2, :], o_den[:, :],
                                      ALU.mult).then_inc(enc_ready, 1)

                def add_out(i):
                    dve.wait_ge(y_psum, b * NT + (i + 1))
                    dve.tensor_tensor(gated_y[:, i % 2, :], psum[:, 7, (i % 2) * C:(i % 2 + 1) * C],
                                      modrow[:, 0, bass.ds(b, 1), :].squeeze(1), ALU.mult).then_inc(y_read, 1)
                    dve.wait_ge(y_read, b * NT + (i + 1))
                    ch.add(dve.tensor_tensor(xrow(i), xrow(i), gated_y[:, i % 2, :], ALU.add))

                for u in range(NTH * NKV):
                    if u == NKV:
                        for i in range(TPH):
                            add_out(i)
                    divide(u)
                for i in range(TPH, NT):
                    add_out(i)
                ch.settle(apart=True)

                for i in range(NT):
                    ch.add(dve.bn_stats(stats2[:, i, :], xrow(i)))
                ch.settle(apart=True)
                ch.add(dve.tensor_copy(curmod2[:, :], modcol[:, 2 * CK:4 * CK, bass.ds(b, 1)].squeeze(2)))
                for i in range(NT):
                    ch.add(dve.bn_aggr(mv2[:, i, :], stats2[:, i, :]))
                ch.settle()
                dve.sem_inc(stats_ready, 1)
                dve.wait_ge(rstd_ready, b + 1)
                for i in range(NT):
                    dve.tensor_scalar(xn[:, i, :], xrow(i), mv2[:, i, 0:1], rstd2[:, i:i + 1],
                                      ALU.subtract, ALU.mult).then_inc(xn_ready, 1)
                nxt = b * NT + NT
                if more:
                    stats_tile(nxt, b + 1)
                for i in range(NT):
                    dve.wait_ge(h_modulated, b * NT + (i + 1))
                    dve.tensor_tensor(hT_parts[:, 1, :, i * P:(i + 1) * P], h_full[:, i % 2, :, :],
                                      hT_parts[:, 0, :, i * P:(i + 1) * P], ALU.subtract).then_inc(hT_ready, 1)
                if more:
                    normalise_tile(nxt)

                dve.wait_ge(escore, b + 1)
                ch.step(dve.tensor_scalar(scores, scores, 1.0, None, ALU.add))
                ch.step(dve.reciprocal(scores, scores))
                sc3 = scores.rearrange("p (t e) -> p t e", t=NT)
                sb3 = sbias.rearrange("p (t e) -> p t e", t=NT)
                ch.step(dve.tensor_tensor(sb3, sc3, bias_sb[:, :].unsqueeze(1).broadcast_to([P, NT, E]), ALU.add))
                sg = sbias.rearrange("p (g e) -> p g e", e=EG)
                hi = tmp[0][:, 0:NT * NG * 4].rearrange("p (g e) -> p g e", e=4)
                lo = tmp[1][:, 0:NT * NG * 4].rearrange("p (g e) -> p g e", e=4)
                ch.add(dve.tensor_tensor(hi, sg[:, :, 0:4], sg[:, :, 4:8], ALU.max))
                ch.step(dve.tensor_tensor(lo, sg[:, :, 0:4], sg[:, :, 4:8], ALU.min))
                for w, off in ((2, 0), (1, 256)):
                    mn = tmp[2][:, off:off + NT * NG * w].rearrange("p (g e) -> p g e", e=w)
                    mx = tmp[2][:, 128 + off:128 + off + NT * NG * w].rearrange("p (g e) -> p g e", e=w)
                    hi2 = tmp[3][:, off:off + NT * NG * w].rearrange("p (g e) -> p g e", e=w)
                    lo2 = tmp[3][:, 128 + off:128 + off + NT * NG * w].rearrange("p (g e) -> p g e", e=w)
                    ch.add(dve.tensor_tensor(hi2, hi[:, :, 0:w], hi[:, :, w:2 * w], ALU.max))
                    ch.add(dve.tensor_tensor(mn, hi[:, :, 0:w], hi[:, :, w:2 * w], ALU.min))
                    ch.step(dve.tensor_tensor(mx, lo[:, :, 0:w], lo[:, :, w:2 * w], ALU.max))
                    ch.step(dve.tensor_tensor(lo2, mn, mx, ALU.max))
                    hi, lo = hi2, lo2
                gs = tmp[2][:, 512:576]
                ch.step(dve.tensor_tensor(gs, hi.squeeze(2), lo.squeeze(2), ALU.add))
                gs2 = gs.rearrange("p (t g) -> p t g", t=NT)
                vi = gs2.unsqueeze(3).broadcast_to([P, NT, NG, NG])
                vj = gs2.unsqueeze(2).broadcast_to([P, NT, NG, NG])
                above = tmp[0][:, 0:512].rearrange("p (t i j) -> p t i j", t=NT, i=NG)
                equal = tmp[1][:, 0:512].rearrange("p (t i j) -> p t i j", t=NT, i=NG)
                ch.add(dve.tensor_tensor(above, vj, vi, ALU.is_gt))
                ch.step(dve.tensor_tensor(equal, vj, vi, ALU.is_equal))
                ch.step(dve.tensor_tensor(equal, equal, before_sb[:, :, :].unsqueeze(1).broadcast_to([P, NT, NG, NG]),
                                          ALU.mult))
                ch.step(dve.tensor_tensor(above, above, equal, ALU.add))
                pen = tmp[3][:, 512:576].rearrange("p (t g) -> p t g", t=NT)
                ch.step(dve.tensor_reduce(pen, above, AX.X, ALU.add))
                ch.step(dve.tensor_scalar(pen, pen, TOPG - 0.5, MASKED, ALU.is_ge, ALU.mult))
                ch.add(dve.tensor_tensor(cand[:, :, 0:E].rearrange("p t (g e) -> p t g e", g=NG),
                                         sbias.rearrange("p (t g e) -> p t g e", t=NT, g=NG),
                                         pen.unsqueeze(3).broadcast_to([P, NT, NG, EG]), ALU.add))
                ch.step(dve.memset(cand[:, :, E:VW], SENTINEL), apart=True)
                best = tmp[0][:, 512:512 + NT * 8].rearrange("p (t k) -> p t k", t=NT)
                for i in range(NT):
                    ch.add(dve.max(best[:, i, :], cand[:, i, 0:E]))
                ch.settle()
                ch.step(dve.memset(best[:, :, TOPK:8], SENTINEL), apart=True)
                for i in range(NT):
                    ch.add(dve.match_replace(cand[:, i, :], best[:, i, :], cand[:, i, :], CHOSEN))
                ch.settle()
                ch.step(dve.scalar_tensor_tensor(out=wdense[:, :, :], in0=cand[:, :, 0:E], scalar=0.5 * CHOSEN, in1=sc3,
                                                 op0=ALU.is_ge, op1=ALU.mult))
                total = tmp[1][:, 512:512 + NT]
                ch.step(dve.tensor_reduce(total, wdense[:, :, :], AX.X, ALU.add))
                ch.step(dve.tensor_scalar(total, total, SUM_EPS, None, ALU.add))
                ch.step(dve.reciprocal(total, total))
                ch.step(dve.tensor_tensor(wdense[:, :, :], wdense[:, :, :], total.unsqueeze(2).broadcast_to([P, NT, E]), ALU.mult))
                ch.step(dve.tensor_scalar(wdense[:, :, :], wdense[:, :, :], RSF, None, ALU.mult))
                dve.sem_inc(w_ready, 1)

                def hidden(hslot, q, slot=None, routed=None, loads=None):
                    if routed is not None:
                        dve.wait_ge(gw_loaded[slot], loads)
                        for g in range(NTH):
                            dve.wait_ge(h_relued, half_of(q, g))
                            dve.wait_ge(hid_ready, half_before(q, g))
                            dve.tensor_tensor(relu_w[:, g, :], relued[:, g, :], gw_ring[:, slot, g * TH:(g + 1) * TH],
                                              ALU.mult).then_inc(weighted, 1)
                    for g in range(NTH):
                        dve.wait_ge(hid_lo, half_before(q, g))
                        if routed is None:
                            dve.wait_ge(h_relued, half_of(q, g))
                            by = relued
                        else:
                            dve.wait_ge(weighted, routed * 2 + (g + 1 + 2 * RING))
                            by = relu_w
                        dve.tensor_tensor(hid_full[:, g, :], relued[:, g, :], by[:, g, :],
                                          ALU.mult).then_inc(hid_ready, 1)
                    for g in range(NTH):
                        dve.wait_ge(hid_hi, half_of(q, g))
                        dve.tensor_tensor(hid_parts[:, 1, hslot, g * TH:(g + 1) * TH], hid_full[:, g, :],
                                          hid_parts[:, 0, hslot, g * TH:(g + 1) * TH],
                                          ALU.subtract).then_inc(hid_lo, 1)

                dve.wait_ge(wT_psum, b + 1)
                dve.tensor_copy(wT_sb, psum[0:E, 2:4, :].rearrange("p a t -> p (a t)")).then_inc(wT_copied, 1)
                hidden(0, b * NQ)
                hidden(1, b * NQ + 1)

                def turn(i, second, first):
                    n = nxt + i
                    for j in range(UNROLL):
                        q = b * NQ + i * UNROLL + (NSH + j)
                        hidden(j % 2, q, j, b * NCH + i * UNROLL + j, b * (TURNS * 32) + i * 32 + 32)
                        if second and j == 0:
                            rotate_tile(n, i)
                        if first and j == 0:
                            stats_tile(n + 1)
                        if first and j == 1:
                            normalise_tile(n + 1)
                        if second and j == 1:
                            split_tile(n)

                with dve.Fori(0, TURNS - 1) as i:
                    turn(i, more, more)
                turn(TURNS - 1, more, False)

                dve.wait_ge(chunk_used, b * NQ + (NQ + FREE))
                for h in range(2):
                    for i in range(h * NT // 2, (h + 1) * NT // 2):
                        ch.step(dve.tensor_tensor(gated_y[:, i % 2, :], psum[:, 4 + i // 2, (i % 2) * C:(i % 2 + 1) * C],
                                                  modrow[:, 1, bass.ds(b, 1), :].squeeze(1), ALU.mult))
                        ch.add(dve.tensor_tensor(xrow(i), xrow(i), gated_y[:, i % 2, :], ALU.add))
                        if i % 2:
                            dve.sem_inc(bank_read, 1)
                    ch.settle()
                    dve.sem_inc(row_done, 1)
                assert ch.n == DVE_ROW, ch.n

            rows(dve, row)


def _rotary_tables():
    fraction = np.arange(0, HD, 2, dtype=np.float32) / np.float32(HD)
    timescale = np.float32(10000.0) ** fraction
    angle = np.arange(T, dtype=np.float32)[:, None] * (np.float32(1.0) / timescale)[None, :]
    return np.cos(angle).astype(np.float32), np.sin(angle).astype(np.float32)


def kernel(L0_attn_x, L0_attn_Wq, L0_attn_Wk, L0_attn_Wv, L0_attn_Wout, L0_ffn_gate_w, L0_ffn_gate_bias,
           L0_ffn_w1, L0_ffn_w2, L0_ffn_shared_up, L0_ffn_shared_down, L0_c, L0_wmod):
    import concourse.bacc as bacc
    from concourse.bass_utils import run_bass_kernel_spmd

    cos, sin = _rotary_tables()
    arrays = {
        "x": np.asarray(L0_attn_x).reshape(B * T, C),
        "cT": np.asarray(L0_c).T,
        "wmod": L0_wmod,
        "wq": L0_attn_Wq, "wk": L0_attn_Wk, "wv": L0_attn_Wv, "wout": L0_attn_Wout,
        "gate_w": np.asarray(L0_ffn_gate_w).T,
        "gate_bias": L0_ffn_gate_bias,
        "w1": np.asarray(L0_ffn_w1).reshape(E * EI, C).T,
        "w2": np.asarray(L0_ffn_w2).transpose(0, 2, 1).reshape(E * EI, C),
        "up": np.asarray(L0_ffn_shared_up).T,
        "down": np.asarray(L0_ffn_shared_down).T,
        "cos": cos, "sin": sin,
        "eye": np.eye(P, dtype=np.float32),
        "before": np.tril(np.ones((NG, NG), np.float32), -1),
    }
    arrays = {f"in_{k}": np.ascontiguousarray(v) for k, v in arrays.items()}
    nc = bacc.Bacc("TRN2", target_bir_lowering=False, num_devices=1)
    args = [nc.dram_tensor(k, v.shape, mybir.dt.from_np(v.dtype), kind="ExternalInput").ap()
            for k, v in arrays.items()]
    args.append(nc.dram_tensor("out", (B * T, C), F32, kind="ExternalOutput").ap())
    adaln_layer(nc, *args)
    r = run_bass_kernel_spmd(nc, [arrays], core_ids=[0])
    return r.results[0]["out"].reshape(B, T, C)
```

```python
from contextlib import ExitStack

import numpy as np

import concourse.bass as bass
from concourse import mybir

F32 = mybir.dt.float32
BF16 = mybir.dt.bfloat16
F32R = mybir.dt.float32r
ALU = mybir.AluOpType
ACT = mybir.ActivationFunctionType
AX = mybir.AxisListType

P = 128
B, T, C = 4, 1024, 256
NT = T // P
CK = C // P
NH, NKV, HD = 16, 4, 16
G = NH // NKV
NQK = NH + NKV
QKV = (NH + 2 * NKV) * HD
HALF = HD // 2
PARTS = 6
KS = PARTS * HD
E, NG, TOPG, TOPK = 64, 8, 4, 6
EG = E // NG
EI = 64
SH = 256
RSF = 2.5
TH = 512
NTH = T // TH
TPH = TH // P
NSH = SH // P
NCH = E * EI // P
NQ = NSH + NCH
RING = 4
UNROLL = RING
FREE = 2
MODS = (0, 1, 3, 4)
TURNS = NCH // UNROLL
assert TURNS == NT
STEPS = NTH * NKV * NT
MASKED, SENTINEL, CHOSEN = -3.0e38, -3.2e38, 3.0e38
LN_EPS, RMS_EPS, SUM_EPS = 1e-5, 1e-6, 1e-20


def hold(eng, held, sem, value):
    eng.wait_ge(sem, value)
    eng.sem_inc(held, 1)


class Chain:

    def __init__(self, eng, sem, held, base=0, row=None, per=0):
        self.eng, self.sem, self.held, self.base, self.row, self.per = eng, sem, held, base, row, per
        self.n = 0

    def add(self, ins):
        ins.then_inc(self.sem, 1)
        self.n += 1

    def settle(self, apart=False):
        k = self.base + self.n
        if self.row is not None:
            k = self.row * self.per + k
        if apart:
            hold(self.eng, self.held, self.sem, k)
        else:
            self.eng.wait_ge(self.sem, k)

    def step(self, ins, apart=False):
        self.add(ins)
        self.settle(apart)


NP = NT // 2
ENC_ROW = NTH * NKV - 1 + TPH
NORM_GROUPS = ((0, TPH), (TPH, TPH + 2), (TPH + 2, NT))
NORM_STEPS = (45, 49)
ROUTE_STEPS = (53, 57)
CLOCK_ALONE = 16
CLOCK_GAPS = (19, 12, 4, 22)
DVE_ROW = 123
POOL_ROW = 3
DVE_TILE = 13
POOL_RMS, POOL_KEYS = 3, 2
EARLY = 2 * C
QKV_BANKS = (3, 4)
PASSES = ((0, 0), (0, 1), (1, 0))


def tile_of(per, n, k=0):
    return n * per + (per + k)


def half_of(q, g):
    return q * NTH + (g + 1 + NTH)


def half_before(q, g):
    return q * NTH + (g + 1)


def adaln_layer(nc, x, cT, wmod, wq, wk, wv, wout, gate_w, gate_bias, w1, w2, up, down, cos, sin,
                eye, parity, out):
    wT = nc.dram_tensor("gate_weights_T", [E, T], F32, kind="Internal").ap()

    with ExitStack() as ctx:
        def sb(name, shape, dt=F32):
            return ctx.enter_context(nc.sbuf_tensor(name, shape, dt))

        def sb_under(name, shape, dt=F32):
            with nc.sbuf_tensor(name, shape, dt) as t:
                return t

        def sem(name):
            return ctx.enter_context(nc.semaphore(name))

        psum = ctx.enter_context(nc.psum_tensor("psum", [P, 8, 512], F32))

        ident = sb("ident", [P, P])
        ident_b = sb("ident_b", [P, P], BF16)
        cos_sb, sin_sb = sb("cos_sb", [P, NT, HALF]), sb("sin_sb", [P, NT, HALF])
        bias_sb = sb("bias_sb", [P, E])
        wqkv_parts = sb("wqkv_parts", [P, 2, CK, QKV], F32R)
        wout_sb = sb("wout_sb", [P, NKV // 2, C])
        own_rows = sb("own_rows", [P, 2])
        gate_parts = sb("gate_parts", [P, 2, CK, E], F32R)
        minus_half = sb("minus_half", [P, NT])
        c_sb = sb("c_sb", [P, CK, B])
        silu = sb("silu", [P, CK, B])
        modcol = sb("modcol", [P, len(MODS) * CK, B])
        modrow = sb("modrow", [P, 2, B, C])
        xs = sb("xs", [P, B * NT, C])
        stats1 = sb("stats1", [P, 6])
        mv1 = sb("mv1", [P, 2])
        rstd1 = sb("rstd1", [P, 1])
        curmod1 = sb("curmod1", [P, 2 * CK])
        xn1 = sb("xn1", [P, C])
        h1_full = sb("h1_full", [P, CK, P])
        h1_parts = sb("h1_parts", [P, 2, CK, P], F32R)
        ssq = sb("ssq", [P, 2])
        rrms = sb("rrms", [P, 2])
        rotary = sb("rotary", [P, 5, NQK * HD])
        qk, rot, rest = rotary[:, 0, :], *(rotary[:, i, :].rearrange("p (h d) -> p h d", h=NQK) for i in (1, 2))
        rope = [rotary[:, 3 + i // 2, (i % 2) * NQK * HALF:(i % 2 + 1) * NQK * HALF].rearrange(
            "p (h d) -> p h d", h=NQK) for i in range(4)]
        wout_gated = rotary[:, :, :].rearrange("p a n -> p (a n)")[:, 0:NKV // 2 * C].rearrange(
            "p (j c) -> p j c", j=NKV // 2)
        stack = sb("stack", [P, NQK, PARTS, HD], BF16)
        QT = sb("QT", [KS, NH, T], BF16)
        KT = sb("KT", [KS, NKV, T], BF16)
        V1 = sb("V1", [P, NT, NKV, 2 * HD])
        probs = sb("probs", [P, 3, G, TH])
        o_sb = sb_under("o_sb", [P, 2, TH])
        w1_parts = sb("w1_parts", [P, 2, 2, CK, P], F32R)
        o_den = sb("o_den", [P, TH])
        encT = sb_under("encT", [P, NKV, T])
        hid_parts = sb("hid_parts", [P, 2, 2, T], F32R)
        gated_y = sb("gated_y", [P, 2, C])
        stats2 = sb("stats2", [P, NT, 6])
        mv2 = sb("mv2", [P, NT, 2])
        rstd2 = sb("rstd2", [P, NT])
        curmod2 = sb("curmod2", [P, 2 * CK])
        xn = sb_under("xn", [P, NT, C])
        relu_w = sb("relu_w", [P, NTH, TH])
        w2_parts = sb("w2_parts", [P, 2, 2, C], F32R)
        h_full0 = sb("h_full0", [P, CK, 2 * P])
        hT_parts = sb("hT_parts", [P, 2, CK, T], F32R)
        VW = E + 2
        cand = sb("cand", [P, NT, VW])
        wdense = sb("wdense", [P, NT, E])
        tmp_all = sb("tmp_all", [P, 4, 576])
        tmp = [tmp_all[:, i, :] for i in range(4)]
        w1_ring = sb("w1_ring", [P, RING, CK, P])
        w2_ring = sb("w2_ring", [P, RING, C])
        flat = probs[:, :, :, :].rearrange("p a g t -> p (a g t)")
        enc_flat = encT[:, :, :].rearrange("p k t -> p (k t)")
        wmod_sb = flat[:, 0:CK * 6 * C].rearrange("p (k n) -> p k n", k=CK)
        siluB = flat[:, CK * 6 * C:CK * 6 * C + CK * B * P].rearrange("p (k b n) -> p k b n", k=CK, b=B)
        rowtmp = enc_flat[:, 0:2 * B * C]
        wqkv_full = enc_flat[:, 2 * B * C:2 * B * C + CK * QKV].rearrange("p (k n) -> p k n", k=CK)
        gate_full = enc_flat[:, 2 * B * C + CK * QKV:2 * B * C + CK * (QKV + E)].rearrange("p (k n) -> p k n", k=CK)
        gw_ring = flat[:, 0:RING * T].rearrange("p (s t) -> p s t", s=RING)
        h_full1 = flat[:, 0:CK * 2 * P].rearrange("p (k n) -> p k n", k=CK)
        h_full = [h_full0, h_full0, h_full0, h_full1]
        relued = flat[:, RING * T:(RING + 1) * T].rearrange("p (g t) -> p g t", g=NTH)
        hid_full = flat[:, (RING + 1) * T:(RING + 2) * T].rearrange("p (g t) -> p g t", g=NTH)
        scores = relu_w[:, 0, :]
        sbias = relu_w[:, 1, :]
        squares = o_den
        exp_T = tmp_all[:, :, :].rearrange("p a t -> p (a t)")[0:E, 0:T].rearrange("p (h t) -> p h t", h=2)
        wT_sb = tmp_all[:, :, :].rearrange("p a t -> p (a t)")[0:E, 0:T]

        x_loaded = sem("x_loaded")
        x_rest_loaded = sem("x_rest_loaded")
        tables_loaded = sem("tables_loaded")
        w_loaded = sem("w_loaded")
        c_loaded = sem("c_loaded")
        wmod_loaded = sem("wmod_loaded")
        wmod_rest_loaded = sem("wmod_rest_loaded")
        qkv_w_loaded = sem("qkv_w_loaded")
        ones_set = sem("ones_set")
        dve_chain = sem("dve_chain")
        tile_chain = sem("tile_chain")
        stat_chain = sem("stat_chain")
        pool_chain = sem("pool_chain")
        pool_rms_chain = sem("pool_rms_chain")
        pool_keys_chain = sem("pool_keys_chain")
        pool_stat_chain = sem("pool_stat_chain")
        held = sem("held")
        held_pool = sem("held_pool")
        held_sp = sem("held_sp")
        held_pe = sem("held_pe")
        consts_set = sem("consts_set")
        silu_exp = sem("silu_exp")
        gates_ready = sem("gates_ready")
        silu_ready = sem("silu_ready")
        mod_cols = sem("mod_cols")
        mod_rows = sem("mod_rows")
        mod_rows_copied = sem("mod_rows_copied")
        mod_cols_copied = sem("mod_cols_copied")
        siluB_ready = sem("siluB_ready")
        qkv_w_split = sem("qkv_w_split")
        mods_set = sem("mods_set")
        p_stats = sem("p_stats")
        p_rstd = sem("p_rstd")
        p_xn = sem("p_xn")
        p_xnT = sem("p_xnT")
        p_mod = sem("p_mod")
        p_h = sem("p_h")
        p_qkv = sem("p_qkv")
        p_squares = sem("p_squares")
        p_v = sem("p_v")
        p_rrms = sem("p_rrms")
        p_parts = sem("p_parts")
        p_qrep = sem("p_qrep")
        p_krep = sem("p_krep")
        p_stackT = sem("p_stackT")
        p_copied = sem("p_copied")
        logits_ready = sem("logits_ready")
        exp_done = sem("exp_done")
        pv_done = sem("pv_done")
        o_copied = sem("o_copied")
        enc_ready = sem("enc_ready")
        y_psum = sem("y_psum")
        y_read = sem("y_read")
        wout_ready = sem("wout_ready")
        stats_ready = sem("stats_ready")
        rstd_ready = sem("rstd_ready")
        xn_ready = sem("xn_ready")
        xnT_ready = sem("xnT_ready")
        h_modulated = sem("h_modulated")
        hT_ready = sem("hT_ready")
        logit_psum = sem("logit_psum")
        escore = sem("escore")
        scores_psum = sem("scores_psum")
        scores_read = sem("scores_read")
        w_ready = sem("w_ready")
        wT_psum = sem("wT_psum")
        wT_copied = sem("wT_copied")
        wT_stored = sem("wT_stored")
        chunk_loaded = [sem(f"chunk_loaded{s}") for s in range(RING)]
        gw_loaded = [sem(f"gw_loaded{s}") for s in range(RING)]
        w1_hi = sem("w1_hi")
        w1_lo = sem("w1_lo")
        w2_hi = sem("w2_hi")
        w2_lo = sem("w2_lo")
        h_psum = sem("h_psum")
        h_relued = sem("h_relued")
        hid_ready = sem("hid_ready")
        hid_hi = sem("hid_hi")
        hid_lo = sem("hid_lo")
        weighted = sem("weighted")
        chunk_used = sem("chunk_used")
        bank_done = sem("bank_done")
        bank_read = sem("bank_read")
        row_done = sem("row_done")
        stored = sem("stored")

        block = ctx.enter_context(nc.Block())

        def rows(eng, row):
            with eng.Fori(0, B - 1) as b:
                row(b, True)
            row(B - 1, False)

        def loads_before(b, i, slot):
            return b * TURNS + i if slot < 2 else b * (TURNS + 1) + i + 1

        @block.sync
        def _(sp):
            wm = wmod.rearrange("(k p) n -> p k n", p=P)
            sp.dma_start(c_sb[:, :, :], cT.rearrange("(k p) b -> p k b", p=P)).then_inc(c_loaded, 16)
            sp.dma_start(wmod_sb[:, :, 0:EARLY], wm[:, :, 0:EARLY]).then_inc(wmod_loaded, 16)
            sp.dma_start(xs[:, 0:NT, :], x[0:T, :].rearrange("(t p) c -> p t c", p=P)).then_inc(x_loaded, 16)
            sp.dma_start(ident[:, :], eye).then_inc(qkv_w_loaded, 16)
            sp.dma_start(wqkv_full[:, :, 0:C], wq.rearrange("(k p) n -> p k n", p=P)).then_inc(qkv_w_loaded, 16)
            sp.dma_start(wqkv_full[:, :, C:C + 64], wk.rearrange("(k p) n -> p k n", p=P)).then_inc(qkv_w_loaded, 16)
            sp.dma_start(wqkv_full[:, :, C + 64:QKV], wv.rearrange("(k p) n -> p k n", p=P)).then_inc(qkv_w_loaded, 16)
            sp.dma_start(cos_sb[:, :, :], cos.rearrange("(t p) f -> p t f", p=P)).then_inc(tables_loaded, 16)
            sp.dma_start(sin_sb[:, :, :], sin.rearrange("(t p) f -> p t f", p=P)).then_inc(tables_loaded, 16)
            sp.dma_start(wmod_sb[:, :, EARLY:6 * C], wm[:, :, EARLY:6 * C]).then_inc(wmod_rest_loaded, 16)
            sp.dma_start(gate_full, gate_w.rearrange("(k p) e -> p k e", p=P)).then_inc(w_loaded, 16)
            sp.dma_start(bias_sb[:, :], gate_bias.unsqueeze(0).broadcast_to([P, E])).then_inc(w_loaded, 16)
            sp.dma_start(own_rows[:, :], parity).then_inc(w_loaded, 16)
            wo = wout.rearrange("(j o g h) c -> g o h j c", j=NKV // 2, o=2, g=G)
            for g in range(G):
                for o in range(2):
                    lo = 32 * g + HD * o
                    sp.dma_start(wout_sb[lo:lo + HD, :, :], wo[g, o]).then_inc(w_loaded, 16)
            sp.dma_start(xs[:, NT:B * NT, :], x[T:B * T, :].rearrange("(t p) c -> p t c", p=P)).then_inc(x_rest_loaded, 16)

            def row(b, more):
                hold(sp, held_sp, w2_lo, b * NQ + FREE)
                for q in range(NSH):
                    sp.dma_start(w1_ring[:, q + 2, :, :],
                                 up[:, q * P:(q + 1) * P].rearrange("(k p) n -> p k n", p=P)
                                 ).then_inc(chunk_loaded[q + 2], 16)
                    sp.dma_start(w2_ring[:, q + 2, :], down[q * P:(q + 1) * P, :]).then_inc(chunk_loaded[q + 2], 16)
                def load_weights(i, j):
                    hold(sp, held_sp, w2_lo, b * NQ + i * UNROLL + (NSH + j - RING + 1 + FREE))
                    sp.dma_start(w1_ring[:, j, :, :],
                                 w1[:, bass.ds(i * UNROLL * P + j * P, P)].rearrange("(k p) n -> p k n", p=P)
                                 ).then_inc(chunk_loaded[j], 16)
                    sp.dma_start(w2_ring[:, j, :], w2[bass.ds(i * UNROLL * P + j * P, P), :]
                                 ).then_inc(chunk_loaded[j], 16)

                def load_turn(i, last):
                    for j in range(UNROLL):
                        hold(sp, held_sp, weighted, b * (2 * NCH) + i * (2 * UNROLL) + (2 * j + 2))
                        for k in range(2):
                            src = wT[bass.ds(i * 2 * UNROLL + (2 * j + k), 1), :].broadcast_to([EI, T])
                            sp.dma_start(gw_ring[EI * k:EI * k + EI, j, :], src).then_inc(gw_loaded[j], 16)
                        if j < NSH:
                            load_weights(i, j + NSH)
                        elif not last:
                            load_weights(i + 1, j - NSH)

                load_weights(0, 0)
                load_weights(0, 1)
                hold(sp, held_sp, wT_copied, b * 2 + 2)
                sp.dma_start(wT, wT_sb).then_inc(wT_stored, 16)
                hold(sp, held_sp, wT_stored, b * 16 + 16)
                with sp.Fori(0, TURNS - 1) as i:
                    load_turn(i, False)
                load_turn(TURNS - 1, True)
                n = 4 if more else 2
                for h in range(0, NT, n):
                    hold(sp, held_sp, row_done, b * NT + (h + n))
                    sp.dma_start(out[bass.ds(b * T + h * P, n * P), :].rearrange("(t p) c -> p t c", p=P),
                                 xs[:, bass.ds(b * NT + h, n), :]).then_inc(stored, 16)

            rows(sp, row)
            hold(sp, held_sp, stored, (B - 1) * 32 + 64)

        @block.tensor
        def _(pe):
            def psum_b(k):
                return psum[:, k, :].bitcast(BF16)

            def keep_clock(bank, n):
                for _ in range(n):
                    pe.matmul(psum[:, bank, :].rearrange("p (a n) -> p a n", a=TPH), ident_b[:, :],
                              ident_b[:, :].unsqueeze(1).broadcast_to([P, TPH, P]), start=True, stop=True)

            def mod_columns(mods):
                for m in mods:
                    for k in range(CK):
                        o = psum[:, 0, (m * CK + k) * B:(m * CK + k + 1) * B]
                        for c in range(CK):
                            lo = MODS[m] * C + k * P
                            mm = pe.matmul(o, wmod_sb[:, c, lo:lo + P], silu[:, c, :],
                                           start=(c == 0), stop=(c == CK - 1))
                mm.then_inc(mod_cols, 1)

            def mod_gate(r, mod):
                for b in range(B):
                    o = psum[:, b // 2, (b % 2) * C:(b % 2 + 1) * C]
                    for c in range(CK):
                        mm = pe.matmul(o, siluB[:, c, b, :], wmod_sb[:, c, mod * C:(mod + 1) * C],
                                       start=(c == 0), stop=(c == CK - 1))
                mm.then_inc(mod_rows, 1)

            pe.wait_ge(wmod_loaded, 16)
            pe.wait_ge(silu_ready, 1)
            mod_columns((0, 1))
            pe.sem_inc(chunk_used, FREE)
            pe.sem_inc(h_psum, NTH)
            pe.sem_inc(p_xnT, 1)
            pe.sem_inc(p_qkv, 1)
            pe.sem_inc(p_stackT, 3)

            def transpose_x(n):
                pe.wait_ge(p_xn, tile_of(1, n, 1))
                pe.wait_ge(p_mod, tile_of(1, n))
                for k in range(CK):
                    mm = pe.transpose(psum[:, 2, k * P:(k + 1) * P], xn1[:, k * P:(k + 1) * P], ident[:, :])
                mm.then_inc(p_xnT, 1)

            def project(n):
                pe.wait_ge(p_copied, tile_of(3, n))
                project_into(n, 3)

            def project_into(n, bank):
                pe.wait_ge(p_h, tile_of(1, n, 1))
                for k in range(CK):
                    for a, c in PASSES:
                        mm = pe.matmul(psum[:, bank, 0:QKV], h1_parts[:, a, k, :], wqkv_parts[:, c, k, :],
                                       start=(k == 0 and (a, c) == PASSES[0]),
                                       stop=(k == CK - 1 and (a, c) == PASSES[-1]))
                mm.then_inc(p_qkv, 1)

            def transpose_stack(bank, heads):
                for i, h in enumerate(heads):
                    mm = pe.transpose(psum_b(bank)[0:KS, i * P:(i + 1) * P],
                                      stack[:, h, :, :].rearrange("p a d -> p (a d)"), ident_b[:, :])
                mm.then_inc(p_stackT, 1)

            def transpose_low(n, bank=3):
                pe.wait_ge(p_parts, tile_of(1, n, 1))
                pe.wait_ge(p_qrep, tile_of(1, n, 1))
                transpose_stack(bank, range(0, 8))

            def transpose_high(n, more):
                pe.wait_ge(p_copied, tile_of(3, n, 1))
                transpose_stack(3, range(8, NH))
                pe.wait_ge(p_krep, tile_of(1, n, 1))
                if more:
                    pe.wait_ge(p_mod, tile_of(1, n + 1, 1))
                transpose_stack(2, range(NH, NQK))

            def project_ahead(n):
                if n >= 2:
                    pe.wait_ge(p_parts, tile_of(1, n - 1))
                project_into(n, QKV_BANKS[n % 2])

            pe.wait_ge(qkv_w_loaded, 64)
            transpose_x(0)
            pe.wait_ge(qkv_w_split, 1)
            project_ahead(0)
            transpose_x(1)
            for i in range(NT):
                if i + 1 < NT:
                    project_ahead(i + 1)
                if i + 2 < NT:
                    transpose_x(i + 2)
                if i == 1:
                    pe.wait_ge(wmod_rest_loaded, 16)
                    mod_columns((2, 3))
                elif i == 2:
                    pe.wait_ge(siluB_ready, 1)
                    pe.wait_ge(mod_cols_copied, 2)
                    mod_gate(0, 2)
                elif i == 3:
                    pe.wait_ge(mod_rows_copied, 1)
                    keep_clock(0, CLOCK_ALONE)
                elif i == 4:
                    mod_gate(1, 5)
                elif i > 4:
                    pe.wait_ge(mod_rows_copied, 2)
                    keep_clock(0, CLOCK_ALONE)
                pe.wait_ge(p_copied, tile_of(3, i))
                transpose_low(i, 5)
                transpose_stack(6, range(8, NH))
                pe.wait_ge(p_krep, tile_of(1, i, 1))
                transpose_stack(7, range(NH, NQK))
            pe.wait_ge(w_loaded, 16 * 11)

            def row(b, more):
                def logits(st, pair):
                    th, kv, s = st // (NKV * NT), st // NT % NKV, st % NT
                    n = 2 * st + pair
                    if n == 2:
                        pe.wait_ge(bank_read, b * NT + 4)
                    if n >= 3:
                        pe.wait_ge(exp_done, b * 2 * STEPS + (n - 2))
                    for k in range(2):
                        mm = pe.matmul(psum[:, 2 * (n % 3) + k, :], KT[:, kv, s * P:(s + 1) * P],
                                       QT[:, kv * G + 2 * pair + k, th * TH:(th + 1) * TH], start=True, stop=True)
                    mm.then_inc(logits_ready, 1)

                def attend(st):
                    kv, s = st // NT % NKV, st % NT
                    if st == 0:
                        pe.wait_ge(bank_read, b * NT + 6)
                    pe.wait_ge(exp_done, b * 2 * STEPS + (2 * st + 2))
                    if s == 0 and st >= NT:
                        pe.wait_ge(o_copied, b * NTH * NKV + st // NT)
                    for g in range(G):
                        mm = pe.matmul(psum[32 * g:32 * g + 32, 6, :], V1[:, s, kv, :], probs[:, st % 3, g, :],
                                       start=(s == 0), stop=(s == NT - 1))
                    mm.then_inc(pv_done, 1)

                def project_out(i, terms):
                    bank, col = (7, (i % 2) * C) if i < TPH else (i - TPH, 0)
                    for k in terms:
                        last = k == (1 if i < TPH else 2)
                        mm = pe.matmul(psum[:, bank, col:col + C], encT[:, k, i * P:(i + 1) * P],
                                       wout_gated[:, min(k, 1), :], start=(k == 0), stop=last)
                    if last:
                        mm.then_inc(y_psum, 1)

                def transpose_pair(p, bank):
                    for ii in range(2):
                        pe.wait_ge(xn_ready, b * NT + (2 * p + ii + 1))
                        for k in range(CK):
                            mm = pe.transpose(psum[:, bank, (2 * k + ii) * P:(2 * k + ii + 1) * P],
                                              xn[:, 2 * p + ii, k * P:(k + 1) * P], ident[:, :])
                    mm.then_inc(xnT_ready, 1)

                def router(h):
                    pe.wait_ge(hT_ready, b * NP + (h + 1) * (NP // 2))
                    for k in range(CK):
                        for a, c in PASSES:
                            mm = pe.matmul(psum[0:E, 7 - h, :], gate_parts[:, a, k, :],
                                           hT_parts[:, c, k, h * TH:(h + 1) * TH],
                                           start=(k == 0 and (a, c) == PASSES[0]),
                                           stop=(k == CK - 1 and (a, c) == PASSES[-1]))
                    mm.then_inc(logit_psum, 1)

                def transpose_scores(h):
                    hold(pe, held_pe, escore, b * 2 + (h + 1))
                    for ii in range(TPH):
                        mm = pe.transpose(psum[:, 7 - h, ii * E:(ii + 1) * E], exp_T[:, h, ii * P:(ii + 1) * P],
                                          ident[0:E, 0:E])
                    mm.then_inc(scores_psum, 1)

                pe.wait_ge(p_copied, tile_of(3, b * NT + (NT - 1), 3))
                pe.wait_ge(p_v, tile_of(1, b * NT + (NT - 1), 1))
                for st in range(STEPS + 1):
                    if st < STEPS:
                        logits(st, 0)
                        logits(st, 1)
                    if st >= 1:
                        attend(st - 1)
                    r = st - NKV * NT - 3
                    if r >= 0 and r < TPH:
                        if r == 0:
                            pe.wait_ge(wout_ready, b + 1)
                            pe.wait_ge(enc_ready, b * ENC_ROW + NKV)
                            pe.wait_ge(bank_read, b * NT + 8)
                        else:
                            pe.wait_ge(y_read, b * NT + r)
                        project_out(r, (0, 1))
                    if st == NORM_STEPS[0]:
                        pe.wait_ge(y_read, b * NT + TPH)
                        transpose_pair(0, 7)
                    if st == NORM_STEPS[1]:
                        pe.wait_ge(h_modulated, b * NP + 1)
                        transpose_pair(1, 7)
                    if st == ROUTE_STEPS[0]:
                        router(0)
                    if st == ROUTE_STEPS[1]:
                        transpose_scores(0)
                pe.wait_ge(enc_ready, b * ENC_ROW + (NTH * NKV - 1))
                for i in range(TPH, NT):
                    project_out(i, (0, 1))
                for i in range(TPH, NT):
                    pe.wait_ge(enc_ready, b * ENC_ROW + (NTH * NKV - 1 + i - TPH + 1))
                    project_out(i, (2,))
                keep_clock(4, CLOCK_GAPS[0])
                transpose_pair(2, 4)
                transpose_pair(3, 5)
                pe.wait_ge(y_read, b * NT + NT)
                keep_clock(3, CLOCK_GAPS[1])
                pe.wait_ge(o_copied, b * NTH * NKV + NTH * NKV)
                router(1)

                def up_chunk(hslot, q):
                    for g in range(NTH):
                        pe.wait_ge(h_relued, half_before(q, g))
                        if g == 0:
                            pe.wait_ge(w1_lo, q + 1)
                        for k in range(CK):
                            for a, c in PASSES:
                                mm = pe.matmul(psum[:, g, :], w1_parts[:, a, hslot, k, :],
                                               hT_parts[:, c, k, g * TH:(g + 1) * TH],
                                               start=(k == 0 and (a, c) == PASSES[0]),
                                               stop=(k == CK - 1 and (a, c) == PASSES[-1]))
                        mm.then_inc(h_psum, 1)

                def down_chunk(hslot, q, first=False, last=False):
                    for i in range(NT):
                        if i == 0:
                            pe.wait_ge(w2_lo, q + (1 + FREE))
                        if i % TPH == 0:
                            pe.wait_ge(hid_lo, half_of(q, i // TPH))
                        for a, c in PASSES:
                            mm = pe.matmul(psum[:, 4 + i // 2, (i % 2) * C:(i % 2 + 1) * C],
                                           hid_parts[:, a, hslot, i * P:(i + 1) * P], w2_parts[:, c, hslot, :],
                                           start=(first and i % 2 == 0 and (a, c) == PASSES[0]), stop=True,
                                           skip_group_check=True)
                        if last and i % 2:
                            mm.then_inc(bank_done, 1)
                    if not last:
                        mm.then_inc(chunk_used, 1)

                keep_clock(3, CLOCK_GAPS[2])
                transpose_scores(1)
                up_chunk(0, b * NQ)
                nxt = b * NT + NT
                if more:
                    transpose_x(nxt)
                up_chunk(1, b * NQ + 1)
                keep_clock(3, CLOCK_GAPS[3])
                hold(pe, held_pe, w_ready, b + 1)
                if more:
                    hold(pe, held_pe, p_mod, tile_of(1, nxt, 1))
                for i in range(NT):
                    mm = pe.transpose(psum[0:E, 2 + i // TPH, (i % TPH) * P:(i % TPH + 1) * P],
                                      wdense[:, i, :], ident[:, :])
                    if i % TPH == TPH - 1:
                        mm.then_inc(wT_psum, 1)
                pe.wait_ge(scores_read, b * 2 + 2)
                down_chunk(0, b * NQ, True)
                hold(pe, held_pe, wT_copied, b * 2 + 2)

                def turn(i, second, first):
                    q = b * NQ + i * UNROLL + NSH
                    n = nxt + i
                    up_chunk(0, q)
                    if second:
                        project(n)
                    down_chunk(1, q - 1)
                    up_chunk(1, q + 1)
                    if first:
                        transpose_x(n + 1)
                    down_chunk(0, q)
                    up_chunk(0, q + 2)
                    down_chunk(1, q + 1)
                    up_chunk(1, q + 3)
                    if second:
                        transpose_low(n)
                    down_chunk(0, q + 2)
                    if second:
                        transpose_high(n, first)

                with pe.Fori(0, TURNS - 1) as i:
                    turn(i, more, more)
                turn(TURNS - 1, more, False)
                down_chunk(1, b * NQ + (NQ - 1), last=True)
                pe.sem_inc(chunk_used, 1)

            rows(pe, row)

        @block.scalar
        def _(act):
            act.wait_ge(c_loaded, 16)
            act.activation(silu[:, :, :], c_sb[:, :, :], ACT.Exp, scale=-1.0).then_inc(silu_exp, 1)
            act.sem_inc(p_mod, 1)
            act.sem_inc(p_squares, 2)
            act.sem_inc(p_v, 1)
            act.sem_inc(p_qrep, 1)
            act.sem_inc(p_copied, 3)
            act.sem_inc(h_relued, NTH)
            act.sem_inc(hid_hi, NTH)

            def modulate_tile(n):
                act.wait_ge(p_xnT, tile_of(1, n, 1))
                act.wait_ge(p_qkv, tile_of(1, n))
                for k in range(CK):
                    for o in (h1_full[:, k, :], h1_parts[:, 0, k, :]):
                        a = act.activation(o, psum[:, 2, k * P:(k + 1) * P], ACT.Identity,
                                           bias=curmod1[:, k:k + 1], scale=curmod1[:, k + CK:k + CK + 1])
                a.then_inc(p_mod, 1)

            def square(n, i, bank=3):
                act.wait_ge(p_qkv, tile_of(1, n, 1))
                for o in range(2):
                    a = act.activation(V_rows[:, bass.ds(i, 1), :, o, o * HD:(o + 1) * HD].squeeze(1),
                                       psum[:, bank, NQK * HD:QKV].rearrange("p (j o d) -> p j o d", o=2, d=HD)[:, :, o, :],
                                       ACT.Copy)
                a.then_inc(p_v, 1)
                act.wait_ge(p_squares, tile_of(2, n))
                act.wait_ge(p_rrms, tile_of(1, n))
                act.activation(squares[:, 0:NH * HD], psum[:, bank, 0:NH * HD], ACT.Square,
                               accum_out=ssq[:, 0:1]).then_inc(p_squares, 1)
                act.activation(squares[:, NH * HD:NQK * HD], psum[:, bank, NH * HD:NQK * HD], ACT.Square,
                               accum_out=ssq[:, 1:2]).then_inc(p_squares, 1)

            def replicate(n):
                act.wait_ge(p_parts, tile_of(1, n, 1))
                for src, dst in ((0, 1), (0, 3), (5, 2)):
                    a = act.activation(stack[:, 0:NH, dst, :], stack[:, 0:NH, src, :], ACT.Copy)
                a.then_inc(p_qrep, 1)

            def copy_stack(n, k, dst, bank):
                act.wait_ge(p_stackT, tile_of(3, n, k))
                h = dst.shape[1]
                act.activation(dst, psum[:, bank, :].bitcast(BF16)[0:KS, 0:h * P].rearrange("p (h t) -> p h t", h=h),
                               ACT.Copy).then_inc(p_copied, 1)

            def copy_low(n, i):
                copy_stack(n, 1, QT[:, 0:8, bass.ds(i * P, P)], 3)

            def copy_high(n, i):
                copy_stack(n, 2, QT[:, 8:16, bass.ds(i * P, P)], 3)
                copy_stack(n, 3, KT[:, :, bass.ds(i * P, P)], 2)

            def copy_gate(r):
                act.wait_ge(mod_rows, r + 1)
                for h in range(2):
                    a = act.activation(modrow[:, r, 2 * h:2 * h + 2, :],
                                       psum[:, h, :].rearrange("p (b c) -> p b c", b=2), ACT.Copy)
                a.then_inc(mod_rows_copied, 1)

            V_rows = V1[:, :, :, :].rearrange("p t (j o) d -> p t j o d", o=2)
            modulate_tile(0)
            act.wait_ge(ones_set, 1)
            square(0, 0, QKV_BANKS[0])
            modulate_tile(1)
            for i in range(NT):
                if i + 1 < NT:
                    square(i + 1, i + 1, QKV_BANKS[(i + 1) % 2])
                if i + 2 < NT:
                    modulate_tile(i + 2)
                if i == 2:
                    copy_gate(0)
                if i == 4:
                    copy_gate(1)
                replicate(i)
                copy_stack(i, 1, QT[:, 0:8, i * P:(i + 1) * P], 5)
                copy_stack(i, 2, QT[:, 8:16, i * P:(i + 1) * P], 6)
                copy_stack(i, 3, KT[:, :, i * P:(i + 1) * P], 7)

            def row(b, more):
                def modulate_pair(p, bank):
                    act.wait_ge(xnT_ready, b * NP + (p + 1))
                    if p:
                        act.wait_ge(hT_ready, b * NP + min(p, 2))
                    for k in range(CK):
                        a = act.activation(h_full[p][:, k, :], psum[:, bank, 2 * k * P:2 * (k + 1) * P], ACT.Identity,
                                           bias=curmod2[:, k:k + 1], scale=curmod2[:, k + CK:k + CK + 1])
                    a.then_inc(h_modulated, 1)

                def expose(h):
                    act.wait_ge(logit_psum, b * 2 + (h + 1))
                    act.activation(exp_T[:, h, :], psum[0:E, 7 - h, :], ACT.Exp,
                                   scale=-1.0).then_inc(escore, 1)

                for st in range(STEPS):
                    for pair in range(2):
                        n = 2 * st + pair
                        act.wait_ge(logits_ready, b * 2 * STEPS + (n + 1))
                        if st >= 3 and pair == 0:
                            act.wait_ge(pv_done, b * STEPS + (st - 2))
                        act.activation(probs[:, st % 3, 2 * pair:2 * pair + 2, :], psum[:, 2 * (n % 3):2 * (n % 3) + 2, :],
                                       ACT.Exp).then_inc(exp_done, 1)
                    if st == NORM_STEPS[0] + 2:
                        modulate_pair(0, 7)
                    if st == NORM_STEPS[1] + 2:
                        modulate_pair(1, 7)
                    if st == ROUTE_STEPS[0] + 2:
                        expose(0)
                def split_w1(hslot, slot, q, loads, first=False):
                    act.wait_ge(chunk_loaded[slot], loads * 32 + 32)
                    if not first:
                        act.wait_ge(h_psum, q * 2)
                    act.activation(w1_parts[:, 0, hslot, :, :], w1_ring[:, slot, :, :], ACT.Copy).then_inc(w1_hi, 1)

                def split_w2(hslot, slot, q, loads):
                    act.wait_ge(chunk_loaded[slot], loads * 32 + 32)
                    act.wait_ge(chunk_used, q + (FREE - 1))
                    act.activation(w2_parts[:, 0, hslot, :], w2_ring[:, slot, :], ACT.Copy).then_inc(w2_hi, 1)

                def relu(q):
                    for g in range(NTH):
                        act.wait_ge(h_psum, half_of(q, g))
                        act.wait_ge(hid_ready, half_before(q, g))
                        act.activation(relued[:, g, :], psum[:, g, :], ACT.Relu).then_inc(h_relued, 1)

                def square_hid(q):
                    for g in range(NTH):
                        act.wait_ge(h_relued, half_of(q, g))
                        act.wait_ge(hid_hi, half_before(q, g))
                        act.wait_ge(hid_lo, half_before(q, g))
                        act.activation(hid_full[:, g, :], relued[:, g, :], ACT.Square).then_inc(hid_ready, 1)

                def split_hid(hslot, q):
                    for g in range(NTH):
                        act.wait_ge(hid_ready, half_of(q, g))
                        if g == 0:
                            act.wait_ge(chunk_used, q + (FREE - 1))
                        act.activation(hid_parts[:, 0, hslot, g * TH:(g + 1) * TH], hid_full[:, g, :],
                                       ACT.Copy).then_inc(hid_hi, 1)

                shared = b * (TURNS + 1)
                modulate_pair(2, 4)
                split_w1(0, 2, b * NQ, shared, True)
                modulate_pair(3, 5)
                split_w1(1, 3, b * NQ + 1, shared, True)
                expose(1)
                nxt = b * NT + NT
                split_w2(0, 2, b * NQ, shared)
                relu(b * NQ)
                if more:
                    modulate_tile(nxt)
                square_hid(b * NQ)
                split_hid(0, b * NQ)
                split_w2(1, 3, b * NQ + 1, shared)
                relu(b * NQ + 1)
                square_hid(b * NQ + 1)
                split_w1(0, 0, b * NQ + NSH, loads_before(b, 0, 0))
                split_hid(1, b * NQ + 1)
                act.wait_ge(wT_psum, b * 2 + 2)
                act.activation(wT_sb[:, TH:T], psum[0:E, 3, :], ACT.Copy).then_inc(wT_copied, 1)

                def turn(i, second, first):
                    n = nxt + i
                    for j in range(UNROLL):
                        q = b * NQ + i * UNROLL + (NSH + j)
                        relu(q)
                        if j < UNROLL - 1:
                            split_w1((j + 1) % 2, j + 1, q + 1, loads_before(b, i, j + 1))
                        elif not (isinstance(i, int) and i == TURNS - 1):
                            split_w1(0, 0, q + 1, loads_before(b, i + 1, 0))
                        split_w2(j % 2, j, q, loads_before(b, i, j))
                        if second and j == 0:
                            square(n, i)
                        if second and j == 2:
                            replicate(n)
                        if second and j == 3:
                            copy_low(n, i)
                        if first and j == 1:
                            modulate_tile(n + 1)
                        split_hid(j % 2, q)
                    if second:
                        copy_high(n, i)

                with act.Fori(0, TURNS - 1) as i:
                    turn(i, more, more)
                turn(TURNS - 1, more, False)

            rows(act, row)

        @block.gpsimd
        def _(pool):
            pool.memset(V1[:, :, :, :], 1.0).then_inc(ones_set, 1)
            pool.memset(minus_half[:, :], -0.5).then_inc(consts_set, 1)
            pool.wait_ge(consts_set, 1)
            pool.sem_inc(p_rstd, 1)
            pool.sem_inc(p_h, 1)
            pool.sem_inc(p_rrms, 1)
            pool.sem_inc(p_krep, 1)
            pool.sem_inc(w2_lo, FREE)

            def rstd_tile(n):
                ch = Chain(pool, pool_stat_chain, held_pool, 0, n, 1)
                hold(pool, held_pool, p_stats, tile_of(1, n, 1))
                ch.step(pool.tensor_scalar(rstd1[:, :], mv1[:, 1:2], LN_EPS, None, ALU.add))
                pool.tensor_tensor(rstd1[:, :], rstd1[:, :], minus_half[:, 0:1], ALU.pow).then_inc(p_rstd, 1)

            def lo_tile(n):
                hold(pool, held_pool, p_mod, tile_of(1, n, 1))
                pool.tensor_tensor(h1_parts[:, 1, :, :], h1_full[:, :, :], h1_parts[:, 0, :, :],
                                   ALU.subtract).then_inc(p_h, 1)

            def rms_tile(n, ahead=False):
                ch = Chain(pool, pool_rms_chain, held_pool, 0, n, POOL_RMS)
                hold(pool, held_pool, p_squares, tile_of(2, n, 2))
                if ahead:
                    hold(pool, held_pool, tile_chain, (n - 1) * DVE_TILE + 2)
                ch.add(pool.tensor_scalar(rrms[:, 0:1], ssq[:, 0:1], 1.0 / (NH * HD), RMS_EPS, ALU.mult, ALU.add))
                ch.step(pool.tensor_scalar(rrms[:, 1:2], ssq[:, 1:2], 1.0 / (NKV * HD), RMS_EPS, ALU.mult, ALU.add))
                ch.step(pool.tensor_tensor(rrms[:, :], rrms[:, :], minus_half[:, 0:2], ALU.pow), apart=True)
                pool.tensor_scalar(rrms[:, 0:1], rrms[:, 0:1], HD ** -0.5, None, ALU.mult).then_inc(p_rrms, 1)
                assert ch.n == POOL_RMS

            def keys_tile(n):
                ch = Chain(pool, pool_keys_chain, held_pool, 0, n, POOL_KEYS)
                hold(pool, held_pool, p_parts, tile_of(1, n, 1))
                for src, dst in ((0, 2), (0, 4)):
                    ch.add(pool.tensor_copy(stack[:, NH:NQK, dst, :], stack[:, NH:NQK, src, :]))
                ch.settle(apart=True)
                pool.tensor_copy(stack[:, NH:NQK, 1, :], stack[:, NH:NQK, 5, :]).then_inc(p_krep, 1)
                assert ch.n == POOL_KEYS

            rstd_tile(0)
            lo_tile(0)
            rstd_tile(1)
            rms_tile(0)
            lo_tile(1)
            for i in range(NT):
                if i + 2 < NT:
                    rstd_tile(i + 2)
                if i + 1 < NT:
                    rms_tile(i + 1, True)
                keys_tile(i)
                if i + 2 < NT:
                    lo_tile(i + 2)

            def row(b, more):
                ch = Chain(pool, pool_chain, held_pool, 0, b, POOL_ROW)
                hold(pool, held_pool, gates_ready, 1)
                hold(pool, held_pool, p_parts, tile_of(1, b * NT + (NT - 1), 1))
                pool.tensor_tensor(wout_gated[:, :, :], wout_sb[:, :, :],
                                   modrow[:, 0, bass.ds(b, 1), :].broadcast_to([P, NKV // 2, C]),
                                   ALU.mult).then_inc(wout_ready, 1)
                for g, (lo, hi) in enumerate(NORM_GROUPS):
                    hold(pool, held_pool, stats_ready, b * 3 + (g + 1))
                    r = rstd2[:, lo:hi]
                    ch.step(pool.tensor_scalar(r, mv2[:, lo:hi, 1], LN_EPS, None, ALU.add))
                    pool.tensor_tensor(r, r, minus_half[:, lo:hi], ALU.pow).then_inc(rstd_ready, 1)
                assert ch.n == POOL_ROW

                def split_w1(hslot, slot, q):
                    hold(pool, held_pool, w1_hi, q + 1)
                    pool.tensor_tensor(w1_parts[:, 1, hslot, :, :], w1_ring[:, slot, :, :], w1_parts[:, 0, hslot, :, :],
                                       ALU.subtract).then_inc(w1_lo, 1)

                def split_w2(hslot, slot, q):
                    hold(pool, held_pool, w2_hi, q + 1)
                    pool.tensor_tensor(w2_parts[:, 1, hslot, :], w2_ring[:, slot, :], w2_parts[:, 0, hslot, :],
                                       ALU.subtract).then_inc(w2_lo, 1)

                def split_hid(hslot, q):
                    for g in range(NTH):
                        hold(pool, held_pool, hid_hi, half_of(q, g))
                        pool.tensor_tensor(hid_parts[:, 1, hslot, g * TH:(g + 1) * TH], hid_full[:, g, :],
                                           hid_parts[:, 0, hslot, g * TH:(g + 1) * TH],
                                           ALU.subtract).then_inc(hid_lo, 1)

                nxt = b * NT + NT
                if more:
                    rstd_tile(nxt)
                split_w1(0, 2, b * NQ)
                split_w1(1, 3, b * NQ + 1)
                split_w2(0, 2, b * NQ)
                if more:
                    lo_tile(nxt)
                split_hid(0, b * NQ)
                split_w2(1, 3, b * NQ + 1)
                split_hid(1, b * NQ + 1)
                split_w1(0, 0, b * NQ + NSH)

                def turn(i, second, first):
                    n = nxt + i
                    for j in range(UNROLL):
                        q = b * NQ + i * UNROLL + (NSH + j)
                        if j < UNROLL - 1 or not (isinstance(i, int) and i == TURNS - 1):
                            split_w1((j + 1) % 2, (j + 1) % RING, q + 1)
                        split_w2(j % 2, j, q)
                        if first and j == 0:
                            rstd_tile(n + 1)
                        if second and j == 0:
                            rms_tile(n)
                        if first and j == 1:
                            lo_tile(n + 1)
                        if second and j == 2:
                            keys_tile(n)

                with pool.Fori(0, TURNS - 1) as i:
                    turn(i, more, more)
                turn(TURNS - 1, more, False)

            rows(pool, row)

        @block.vector
        def _(dve):
            su = Chain(dve, dve_chain, held)
            dve.sem_inc(p_stats, 1)
            dve.sem_inc(p_xn, 1)
            dve.sem_inc(p_parts, 1)
            dve.sem_inc(hid_ready, NTH)
            dve.sem_inc(hid_lo, NTH)
            dve.sem_inc(weighted, 2 * RING)
            dve.sem_inc(bank_read, NT)
            dve.wait_ge(silu_exp, 1)
            su.step(dve.tensor_scalar(silu[:, :, :], silu[:, :, :], 1.0, None, ALU.add))
            su.step(dve.reciprocal(silu[:, :, :], silu[:, :, :]))
            su.step(dve.tensor_tensor(silu[:, :, :], silu[:, :, :], c_sb[:, :, :], ALU.mult))
            su.settle()
            dve.sem_inc(silu_ready, 1)

            def take_columns(mods, which):
                dve.wait_ge(mod_cols, which)
                lo, hi = mods[0] * CK * B, (mods[-1] + 1) * CK * B
                su.step(dve.tensor_copy(modcol[:, :, :].rearrange("p m b -> p (m b)")[:, lo:hi], psum[:, 0, lo:hi]))
                dve.sem_inc(mod_cols_copied, 1)
                v = modcol[:, mods[1] * CK:(mods[1] + 1) * CK, :]
                su.step(dve.tensor_scalar(v, v, 1.0, None, ALU.add))

            def stats_tile(n, b=None):
                ch = Chain(dve, stat_chain, held, 0, n, 2)
                hold(dve, held, p_xn, tile_of(1, n))
                ch.add(dve.bn_stats(stats1[:, :], xs[:, bass.ds(n, 1), :].squeeze(1)))
                if b is not None:
                    hold(dve, held, p_mod, tile_of(1, n))
                    dve.tensor_copy(curmod1[:, :], modcol[:, 0:2 * CK, bass.ds(b, 1)].squeeze(2)).then_inc(mods_set, 1)
                ch.settle(apart=True)
                ch.step(dve.bn_aggr(mv1[:, :], stats1[:, :]))
                if b is not None:
                    dve.wait_ge(mods_set, b + 1)
                dve.sem_inc(p_stats, 1)

            def normalise_tile(n):
                dve.wait_ge(p_rstd, tile_of(1, n, 1))
                dve.wait_ge(p_xnT, tile_of(1, n))
                dve.tensor_scalar(xn1[:, :], xs[:, bass.ds(n, 1), :].squeeze(1), mv1[:, 0:1], rstd1[:, 0:1],
                                  ALU.subtract, ALU.mult).then_inc(p_xn, 1)

            def rotate_tile(n, i, bank=3):
                ch = Chain(dve, tile_chain, held, 0, n, DVE_TILE)
                dve.wait_ge(p_rrms, tile_of(1, n, 1))
                ch.add(dve.tensor_scalar(qk[:, 0:NH * HD], psum[:, bank, 0:NH * HD], rrms[:, 0:1], None, ALU.mult))
                ch.step(dve.tensor_scalar(qk[:, NH * HD:NQK * HD], psum[:, bank, NH * HD:NQK * HD], rrms[:, 1:2], None,
                                          ALU.mult))
                v = qk.rearrange("p (h d) -> p h d", h=NQK)
                cs = cos_sb[:, bass.ds(i, 1), :].broadcast_to([P, NQK, HALF])
                sn = sin_sb[:, bass.ds(i, 1), :].broadcast_to([P, NQK, HALF])
                for r, (part, tab) in enumerate(((0, cs), (1, sn), (1, cs), (0, sn))):
                    ch.add(dve.tensor_tensor(rope[r][:, :, :], v[:, :, part * HALF:(part + 1) * HALF], tab, ALU.mult))
                return ch

            def split_tile(n):
                ch = Chain(dve, tile_chain, held, 6, n, DVE_TILE)
                ch.settle()
                ch.add(dve.tensor_tensor(rot[:, :, 0:HALF], rope[0][:, :, :], rope[1][:, :, :], ALU.subtract))
                ch.step(dve.tensor_tensor(rot[:, :, HALF:HD], rope[2][:, :, :], rope[3][:, :, :], ALU.add))
                dve.wait_ge(p_stackT, tile_of(3, n))
                ch.step(dve.tensor_copy(stack[:, :, 0, :], rot[:, :, :]))
                ch.step(dve.tensor_tensor(rest[:, :, :], rot[:, :, :], stack[:, :, 0, :], ALU.subtract))
                ch.step(dve.tensor_copy(stack[:, :, 5, :], rest[:, :, :]))
                ch.add(dve.tensor_tensor(stack[:, 0:NH, 4, :], rest[:, 0:NH, :], stack[:, 0:NH, 5, :], ALU.subtract))
                ch.step(dve.tensor_tensor(stack[:, NH:NQK, 3, :], rest[:, NH:NQK, :], stack[:, NH:NQK, 5, :],
                                          ALU.subtract))
                dve.sem_inc(p_parts, 1)
                assert 6 + ch.n == DVE_TILE

            take_columns((0, 1), 1)
            dve.wait_ge(x_loaded, 16)
            stats_tile(0, 0)
            dve.wait_ge(qkv_w_loaded, 64)
            su.step(dve.tensor_copy(wqkv_parts[:, 0, :, :], wqkv_full))
            normalise_tile(0)
            su.add(dve.tensor_tensor(wqkv_parts[:, 1, :, :], wqkv_full, wqkv_parts[:, 0, :, :], ALU.subtract))
            su.add(dve.tensor_copy(ident_b[:, :], ident[:, :]))
            su.settle()
            dve.sem_inc(qkv_w_split, 1)
            stats_tile(1)
            normalise_tile(1)
            su.step(dve.tensor_copy(siluB.rearrange("p k b n -> p (k b) n"),
                                    silu[:, :, :].rearrange("p k b -> p (k b)").unsqueeze(2).broadcast_to([P, CK * B, P])))
            dve.sem_inc(siluB_ready, 1)
            dve.wait_ge(tables_loaded, 32)
            for i in range(NT):
                if i == 2:
                    take_columns((2, 3), 2)
                if i + 2 < NT:
                    stats_tile(i + 2)
                rotate_tile(i, i, QKV_BANKS[i % 2])
                if i + 2 < NT:
                    normalise_tile(i + 2)
                split_tile(i)
            dve.wait_ge(mod_rows_copied, 2)
            g = modrow[:, :, :, :].rearrange("p r b c -> p (r b c)")
            su.step(dve.tensor_scalar(rowtmp, g, 0.0, 2.0, ALU.is_ge, ALU.mult))
            su.step(dve.tensor_scalar(rowtmp, rowtmp, -1.0, None, ALU.add))
            su.step(dve.tensor_tensor(g, rowtmp, g, ALU.mult))
            su.step(dve.scalar_tensor_tensor(out=g, in0=g, scalar=0.25, in1=rowtmp, op0=ALU.max, op1=ALU.mult))
            dve.wait_ge(w_loaded, 16 * 11)
            dve.sem_inc(gates_ready, 1)
            su.step(dve.tensor_copy(gate_parts[:, 0, :, :], gate_full))
            su.step(dve.tensor_tensor(gate_parts[:, 1, :, :], gate_full, gate_parts[:, 0, :, :], ALU.subtract))
            dve.wait_ge(x_rest_loaded, 16)
            dve_setup = su.n

            def row(b, more):
                ch = Chain(dve, dve_chain, held, dve_setup, b, DVE_ROW)

                def xrow(i):
                    return xs[:, bass.ds(b * NT + i, 1), :].squeeze(1)

                def divide(u):
                    th, kv = u // NKV, u % NKV
                    dve.wait_ge(pv_done, b * STEPS + (u + 1) * NT)
                    dve.tensor_copy(o_sb[:, u % 2, :], psum[:, 6, :]).then_inc(o_copied, 1)
                    hold(dve, held, o_copied, b * NTH * NKV + (u + 1))
                    odd, last = kv % 2, u == NTH * NKV - 1
                    ch.step(dve.stream_shuffle(o_den[:, :], o_sb[:, u % 2, :], [0 if odd else HD] * 32))
                    w = P if last else TH
                    for a in range(0, TH, w):
                        ch.step(dve.reciprocal(o_den[:, a:a + w], o_den[:, a:a + w]))
                        o = o_sb[:, u % 2, a:a + w]
                        pair = encT[:, 2 if last else kv // 2, th * TH + a:th * TH + a + w]
                        d = dve.scalar_tensor_tensor(out=o if odd and not last else pair, in0=o,
                                                     scalar=own_rows[:, odd:odd + 1], in1=o_den[:, a:a + w],
                                                     op0=ALU.mult, op1=ALU.mult)
                        if odd and not last:
                            ch.step(d)
                            d = dve.tensor_tensor(pair, pair, o, ALU.add)
                        d.then_inc(enc_ready, 1)

                def add_out(i):
                    bank, col = (7, (i % 2) * C) if i < TPH else (i - TPH, 0)
                    dve.wait_ge(y_psum, b * NT + (i + 1))
                    dve.tensor_tensor(xrow(i), xrow(i), psum[:, bank, col:col + C], ALU.add).then_inc(y_read, 1)

                def norm_stats(lo, hi):
                    hold(dve, held, y_read, b * NT + hi)
                    for i in range(lo, hi):
                        ch.add(dve.bn_stats(stats2[:, i, :], xrow(i)))
                    ch.settle(apart=True)
                    if lo == 0:
                        ch.add(dve.tensor_copy(curmod2[:, :], modcol[:, 2 * CK:4 * CK, bass.ds(b, 1)].squeeze(2)))
                    for i in range(lo, hi):
                        ch.add(dve.bn_aggr(mv2[:, i, :], stats2[:, i, :]))
                    ch.settle()
                    dve.sem_inc(stats_ready, 1)

                def normalise(g):
                    dve.wait_ge(rstd_ready, b * 3 + (g + 1))
                    for i in range(*NORM_GROUPS[g]):
                        dve.tensor_scalar(xn[:, i, :], xrow(i), mv2[:, i, 0:1], rstd2[:, i:i + 1],
                                          ALU.subtract, ALU.mult).then_inc(xn_ready, 1)

                def split_pair(p):
                    hi, lo = (hT_parts[:, a, :, 2 * p * P:2 * (p + 1) * P] for a in range(2))
                    dve.wait_ge(h_modulated, b * NP + (p + 1))
                    ch.step(dve.tensor_copy(hi, h_full[p][:, :, :]))
                    dve.tensor_tensor(lo, h_full[p][:, :, :], hi, ALU.subtract).then_inc(hT_ready, 1)

                def sigmoid(h):
                    s = slice(h * TPH * E, (h + 1) * TPH * E)
                    dve.wait_ge(scores_psum, b * 2 + (h + 1))
                    dve.tensor_scalar(scores[:, s], psum[:, 7 - h, 0:TPH * E], 1.0, None,
                                      ALU.add).then_inc(scores_read, 1)
                    dve.wait_ge(scores_read, b * 2 + (h + 1))
                    ch.step(dve.reciprocal(scores[:, s], scores[:, s]))
                    ch.add(dve.tensor_tensor(sbias[:, s].rearrange("p (t e) -> p t e", t=TPH),
                                             scores[:, s].rearrange("p (t e) -> p t e", t=TPH),
                                             bias_sb[:, :].unsqueeze(1).broadcast_to([P, TPH, E]), ALU.add))

                def route(h):
                    t0, tiles = h * TPH, slice(h * TPH, (h + 1) * TPH)
                    sc3 = scores[:, h * TPH * E:(h + 1) * TPH * E].rearrange("p (t e) -> p t e", t=TPH)
                    sb_h = sbias[:, h * TPH * E:(h + 1) * TPH * E]
                    ch.settle()
                    sg = sb_h.rearrange("p (g e) -> p g e", e=EG)
                    hi = tmp[0][:, 0:TPH * NG * 4].rearrange("p (g e) -> p g e", e=4)
                    lo = tmp[1][:, 0:TPH * NG * 4].rearrange("p (g e) -> p g e", e=4)
                    ch.add(dve.tensor_tensor(hi, sg[:, :, 0:4], sg[:, :, 4:8], ALU.max))
                    ch.step(dve.tensor_tensor(lo, sg[:, :, 0:4], sg[:, :, 4:8], ALU.min))
                    for w, off in ((2, 0), (1, 256)):
                        mn = tmp[2][:, off:off + TPH * NG * w].rearrange("p (g e) -> p g e", e=w)
                        mx = tmp[2][:, 128 + off:128 + off + TPH * NG * w].rearrange("p (g e) -> p g e", e=w)
                        hi2 = tmp[3][:, off:off + TPH * NG * w].rearrange("p (g e) -> p g e", e=w)
                        lo2 = tmp[3][:, 128 + off:128 + off + TPH * NG * w].rearrange("p (g e) -> p g e", e=w)
                        ch.add(dve.tensor_tensor(hi2, hi[:, :, 0:w], hi[:, :, w:2 * w], ALU.max))
                        ch.add(dve.tensor_tensor(mn, hi[:, :, 0:w], hi[:, :, w:2 * w], ALU.min))
                        ch.step(dve.tensor_tensor(mx, lo[:, :, 0:w], lo[:, :, w:2 * w], ALU.max))
                        ch.step(dve.tensor_tensor(lo2, mn, mx, ALU.max))
                        hi, lo = hi2, lo2
                    GW = NG + 8 - TOPG
                    gcand = tmp[0][:, 0:TPH * GW].rearrange("p (t v) -> p t v", t=TPH)
                    ch.add(dve.tensor_tensor(gcand[:, :, 0:NG], hi.squeeze(2).rearrange("p (t g) -> p t g", t=TPH),
                                             lo.squeeze(2).rearrange("p (t g) -> p t g", t=TPH), ALU.add))
                    ch.step(dve.memset(gcand[:, :, NG:GW], SENTINEL), apart=True)
                    gbest = tmp[1][:, 512:512 + TPH * 8].rearrange("p (t k) -> p t k", t=TPH)
                    for i in range(TPH):
                        ch.add(dve.max(gbest[:, i, :], gcand[:, i, 0:NG]))
                    ch.settle()
                    ch.step(dve.memset(gbest[:, :, TOPG:8], SENTINEL), apart=True)
                    for i in range(TPH):
                        ch.add(dve.match_replace(gcand[:, i, :], gbest[:, i, :], gcand[:, i, :], CHOSEN))
                    ch.settle()
                    pen = tmp[3][:, 512:512 + TPH * NG].rearrange("p (t g) -> p t g", t=TPH)
                    ch.step(dve.tensor_scalar(pen, gcand[:, :, 0:NG], 0.5 * CHOSEN, MASKED, ALU.is_lt, ALU.mult))
                    ch.add(dve.tensor_tensor(cand[:, tiles, 0:E].rearrange("p t (g e) -> p t g e", g=NG),
                                             sb_h.rearrange("p (t g e) -> p t g e", t=TPH, g=NG),
                                             pen.unsqueeze(3).broadcast_to([P, TPH, NG, EG]), ALU.add))
                    ch.step(dve.memset(cand[:, tiles, E:VW], SENTINEL), apart=True)
                    best = tmp[0][:, 512:512 + TPH * 8].rearrange("p (t k) -> p t k", t=TPH)
                    for i in range(TPH):
                        ch.add(dve.max(best[:, i, :], cand[:, t0 + i, 0:E]))
                    ch.settle()
                    ch.step(dve.memset(best[:, :, TOPK:8], SENTINEL), apart=True)
                    for i in range(TPH):
                        ch.add(dve.match_replace(cand[:, t0 + i, :], best[:, i, :], cand[:, t0 + i, :], CHOSEN))
                    ch.settle()
                    ch.step(dve.scalar_tensor_tensor(out=wdense[:, tiles, :], in0=cand[:, tiles, 0:E], scalar=0.5 * CHOSEN, in1=sc3,
                                                     op0=ALU.is_ge, op1=ALU.mult))
                    total = tmp[1][:, 512:512 + TPH]
                    ch.step(dve.tensor_reduce(total, wdense[:, tiles, :], AX.X, ALU.add))
                    ch.step(dve.tensor_scalar(total, total, SUM_EPS, None, ALU.add))
                    ch.step(dve.reciprocal(total, total))
                    ch.step(dve.scalar_tensor_tensor(out=wdense[:, tiles, :], in0=wdense[:, tiles, :], scalar=RSF,
                                                     in1=total.unsqueeze(2).broadcast_to([P, TPH, E]),
                                                     op0=ALU.mult, op1=ALU.mult))

                for u in range(NTH * NKV - 1):
                    if u == NKV:
                        for i in range(TPH):
                            add_out(i)
                        norm_stats(0, TPH)
                    divide(u)
                    if u == NKV:
                        normalise(0)
                        split_pair(0)
                    if u == NKV + 1:
                        split_pair(1)
                    if u == NKV + 2:
                        sigmoid(0)
                        route(0)
                divide(NTH * NKV - 1)
                for lo, hi in NORM_GROUPS[1:]:
                    for i in range(lo, hi):
                        add_out(i)
                    norm_stats(lo, hi)
                normalise(1)
                normalise(2)
                nxt = b * NT + NT
                split_pair(2)
                split_pair(3)
                if more:
                    stats_tile(nxt, b + 1)
                    normalise_tile(nxt)
                sigmoid(1)
                route(1)

                dve.sem_inc(w_ready, 1)

                def hidden(hslot, q, slot, routed, loads):
                    dve.wait_ge(gw_loaded[slot], loads)
                    for g in range(NTH):
                        dve.wait_ge(h_relued, half_of(q, g))
                        dve.wait_ge(hid_ready, half_before(q, g))
                        dve.tensor_tensor(relu_w[:, g, :], relued[:, g, :], gw_ring[:, slot, g * TH:(g + 1) * TH],
                                          ALU.mult).then_inc(weighted, 1)
                    for g in range(NTH):
                        dve.wait_ge(hid_lo, half_before(q, g))
                        dve.wait_ge(weighted, routed * 2 + (g + 1 + 2 * RING))
                        dve.tensor_tensor(hid_full[:, g, :], relued[:, g, :], relu_w[:, g, :],
                                          ALU.mult).then_inc(hid_ready, 1)
                    for g in range(NTH):
                        dve.wait_ge(hid_hi, half_of(q, g))
                        dve.tensor_tensor(hid_parts[:, 1, hslot, g * TH:(g + 1) * TH], hid_full[:, g, :],
                                          hid_parts[:, 0, hslot, g * TH:(g + 1) * TH],
                                          ALU.subtract).then_inc(hid_lo, 1)

                dve.wait_ge(wT_psum, b * 2 + 1)
                dve.tensor_copy(wT_sb[:, 0:TH], psum[0:E, 2, :]).then_inc(wT_copied, 1)

                def turn(i, second, first):
                    n = nxt + i
                    for j in range(UNROLL):
                        q = b * NQ + i * UNROLL + (NSH + j)
                        if first and j == 0:
                            stats_tile(n + 1)
                        hidden(j % 2, q, j, b * NCH + i * UNROLL + j, b * (TURNS * 32) + i * 32 + 32)
                        if first and j == 0:
                            normalise_tile(n + 1)
                        if second and j == 0:
                            rotate_tile(n, i)
                        if second and j == 1:
                            split_tile(n)

                with dve.Fori(0, TURNS - 1) as i:
                    turn(i, more, more)
                turn(TURNS - 1, more, False)

                for k in range(NT // 2):
                    dve.wait_ge(bank_done, b * (NT // 2) + (k + 1))
                    for j in range(2):
                        i = 2 * k + j
                        dve.tensor_tensor(gated_y[:, j, :], psum[:, 4 + k, j * C:(j + 1) * C],
                                          modrow[:, 1, bass.ds(b, 1), :].squeeze(1), ALU.mult).then_inc(bank_read, 1)
                    for j in range(2):
                        i = 2 * k + j
                        dve.wait_ge(bank_read, b * NT + (NT + i + 1))
                        dve.tensor_tensor(xrow(i), xrow(i), gated_y[:, j, :], ALU.add).then_inc(row_done, 1)
                    if k + 1 < NT // 2:
                        hold(dve, held, row_done, b * NT + (2 * k + 2))
                assert ch.n == DVE_ROW, ch.n

            rows(dve, row)


def _rotary_tables():
    fraction = np.arange(0, HD, 2, dtype=np.float32) / np.float32(HD)
    timescale = np.float32(10000.0) ** fraction
    angle = np.arange(T, dtype=np.float32)[:, None] * (np.float32(1.0) / timescale)[None, :]
    return np.cos(angle).astype(np.float32), np.sin(angle).astype(np.float32)


def kernel(L0_attn_x, L0_attn_Wq, L0_attn_Wk, L0_attn_Wv, L0_attn_Wout, L0_ffn_gate_w, L0_ffn_gate_bias,
           L0_ffn_w1, L0_ffn_w2, L0_ffn_shared_up, L0_ffn_shared_down, L0_c, L0_wmod):
    import concourse.bacc as bacc
    from concourse.bass_utils import run_bass_kernel_spmd

    cos, sin = _rotary_tables()
    arrays = {
        "x": np.asarray(L0_attn_x).reshape(B * T, C),
        "cT": np.asarray(L0_c).T,
        "wmod": L0_wmod,
        "wq": L0_attn_Wq, "wk": L0_attn_Wk, "wv": L0_attn_Wv, "wout": L0_attn_Wout,
        "gate_w": np.asarray(L0_ffn_gate_w).T,
        "gate_bias": L0_ffn_gate_bias,
        "w1": np.asarray(L0_ffn_w1).reshape(E * EI, C).T,
        "w2": np.asarray(L0_ffn_w2).transpose(0, 2, 1).reshape(E * EI, C),
        "up": np.asarray(L0_ffn_shared_up).T,
        "down": np.asarray(L0_ffn_shared_down).T,
        "cos": cos, "sin": sin,
        "eye": np.eye(P, dtype=np.float32),
        "parity": np.stack([np.arange(P) // HD % 2 == o for o in range(2)], 1).astype(np.float32),
    }
    arrays = {f"in_{k}": np.ascontiguousarray(v) for k, v in arrays.items()}
    nc = bacc.Bacc("TRN2", target_bir_lowering=False, num_devices=1)
    args = [nc.dram_tensor(k, v.shape, mybir.dt.from_np(v.dtype), kind="ExternalInput").ap()
            for k, v in arrays.items()]
    args.append(nc.dram_tensor("out", (B * T, C), F32, kind="ExternalOutput").ap())
    adaln_layer(nc, *args)
    r = run_bass_kernel_spmd(nc, [arrays], core_ids=[0])
    return r.results[0]["out"].reshape(B, T, C)
```
